# Optimizing a Trainium2 kernel written in Bass

```python
import numpy as np
import jax
import jax.numpy as jnp

def _softmax(x, axis=-1):
    return jax.nn.softmax(x, axis=axis)

def _gelu(x):
    return jax.nn.gelu(x, approximate=True)

def _silu(x):
    return jax.nn.silu(x)

def _sigmoid(x):
    return jax.nn.sigmoid(x)

def _layernorm(x, axis=-1, eps=1e-05):
    m = jnp.mean(x, axis=axis, keepdims=True)
    v = jnp.var(x, axis=axis, keepdims=True)
    return (x - m) / jnp.sqrt(v + eps)

def _scatter_add(tgt, idx, src, axis=0):
    return tgt.at[idx].add(src)

def _segment_sum(src, seg, n):
    return jax.ops.segment_sum(src, seg, n)
kernel_name = 'mk_cond_seq_d2_seqx_r4_ef5251'

def setup_inputs(seed: int=0):
    np.random.seed(seed)
    _w = jnp.asarray

    def _rec_inputs():
        import jax
        import jax.numpy as jnp
        _rk = jax.random.key(seed)
        x = 7.22e-05 + 1 * jax.random.normal(jax.random.fold_in(_rk, 1), (64, 64, 256), jnp.float32)
        _lenS = 64 - jax.random.randint(jax.random.fold_in(_rk, 7), (64,), 0, max(1, 64 // 4) + 1, jnp.int32)
        _lenS2 = 64 - jax.random.randint(jax.random.fold_in(_rk, 8), (64,), 0, max(1, 64 // 4) + 1, jnp.int32)
        cond_1024 = 0.00782532 + 1.00527 * jax.random.normal(jax.random.fold_in(_rk, 11), (64, 256), jnp.float32)
        return (x, cond_1024)
    x, cond_1024 = _rec_inputs()

    def _L0_cond_setup():
        import jax, jax.numpy as jnp
        import numpy as np
        HID = 256
        HEADS = 16
        HEAD_DIM = HID // HEADS
        MLP_HID = 1024
        TEMB = 256
        EPS = 1e-06

        def _ln(x):
            mu = jnp.mean(x, axis=-1, keepdims=True)
            var = jnp.var(x, axis=-1, keepdims=True)
            return (x - mu) * jax.lax.rsqrt(var + EPS)

        def _modulate(x, shift, scale):
            return x * (1.0 + scale[:, None, :]) + shift[:, None, :]

        def _attn(x, W_qkv, b_qkv, W_proj, b_proj):
            B, N, C = x.shape
            qkv = x @ W_qkv + b_qkv
            qkv = qkv.reshape(B, N, 3, HEADS, HEAD_DIM)
            q, k, v = (qkv[:, :, 0], qkv[:, :, 1], qkv[:, :, 2])
            scale = HEAD_DIM ** (-0.5)
            logits = jnp.einsum('bnhd,bmhd->bhnm', q, k) * scale
            attn = jax.nn.softmax(logits, axis=-1)
            out = jnp.einsum('bhnm,bmhd->bnhd', attn, v).reshape(B, N, C)
            return out @ W_proj + b_proj
        key = jax.random.key(seed)
        ks = jax.random.split(key, 12)
        s = 0.02
        return {'x': jax.random.normal(ks[0], (8, 256, HID), jnp.float32), 'c': jax.random.normal(ks[1], (8, TEMB), jnp.float32), 'W_qkv': jax.random.normal(ks[2], (HID, 3 * HID), jnp.float32) * s, 'b_qkv': jnp.zeros((3 * HID,), jnp.float32), 'W_proj': jax.random.normal(ks[3], (HID, HID), jnp.float32) * s, 'b_proj': jnp.zeros((HID,), jnp.float32), 'W_fc1': jax.random.normal(ks[4], (HID, MLP_HID), jnp.float32) * s, 'b_fc1': jnp.zeros((MLP_HID,), jnp.float32), 'W_fc2': jax.random.normal(ks[5], (MLP_HID, HID), jnp.float32) * s, 'b_fc2': jnp.zeros((HID,), jnp.float32), 'W_ada': jax.random.normal(ks[6], (TEMB, 6 * HID), jnp.float32) * s, 'b_ada': jnp.zeros((6 * HID,), jnp.float32)}
    _L0_cond_all = _L0_cond_setup()
    _L0_cond_in = {k: v for k, v in _L0_cond_all.items() if k in ('W_qkv', 'b_qkv', 'W_proj', 'b_proj', 'W_fc1', 'b_fc1', 'W_fc2', 'b_fc2', 'W_ada', 'b_ada')}
    del _L0_cond_all

    def _L1_cond_setup():
        import jax, jax.numpy as jnp
        import numpy as np
        EPS_RMS = 1e-06
        EPS_Q = 1e-05

        def _weight_quant(w):
            scale = 1.0 / jnp.clip(jnp.mean(jnp.abs(w)), EPS_Q)
            wq = jnp.clip(jnp.round(w * scale), -1.0, 1.0) / scale
            return w + jax.lax.stop_gradient(wq - w)

        def _activation_quant(x):
            scale = 127.0 / jnp.clip(jnp.max(jnp.abs(x), axis=-1, keepdims=True), EPS_Q)
            xq = jnp.clip(jnp.round(x * scale), -128.0, 127.0) / scale
            return x + jax.lax.stop_gradient(xq - x)

        def _rmsnorm(x, weight):
            inv = jax.lax.rsqrt(jnp.mean(x * x, axis=-1, keepdims=True) + EPS_RMS)
            return x * inv * weight
        key = jax.random.key(seed)
        k1, k2, k3 = jax.random.split(key, 3)
        B, S, D, CD = (8, 1024, 256, 256)
        x = jax.random.normal(k1, (B, S, D), dtype=jnp.float32)
        c = jax.random.normal(k2, (B, CD), dtype=jnp.float32)
        w_proj = jax.random.normal(k3, (2 * D, CD), dtype=jnp.float32) * 0.02
        b_proj = jnp.zeros((2 * D,), dtype=jnp.float32)
        rms_weight = jnp.ones((D,), dtype=jnp.float32)
        return {'x': x, 'c': c, 'w_proj': w_proj, 'b_proj': b_proj, 'rms_weight': rms_weight}
    _L1_cond_all = _L1_cond_setup()
    _L1_cond_in = {k: v for k, v in _L1_cond_all.items() if k in ('w_proj', 'b_proj', 'rms_weight')}
    del _L1_cond_all
    return {'x': x, 'cond_1024': cond_1024, 'L0_cond_W_qkv': _L0_cond_in['W_qkv'], 'L0_cond_b_qkv': _L0_cond_in['b_qkv'], 'L0_cond_W_proj': _L0_cond_in['W_proj'], 'L0_cond_b_proj': _L0_cond_in['b_proj'], 'L0_cond_W_fc1': _L0_cond_in['W_fc1'], 'L0_cond_b_fc1': _L0_cond_in['b_fc1'], 'L0_cond_W_fc2': _L0_cond_in['W_fc2'], 'L0_cond_b_fc2': _L0_cond_in['b_fc2'], 'L0_cond_W_ada': _L0_cond_in['W_ada'], 'L0_cond_b_ada': _L0_cond_in['b_ada'], 'L1_cond_w_proj': _L1_cond_in['w_proj'], 'L1_cond_b_proj': _L1_cond_in['b_proj'], 'L1_cond_rms_weight': _L1_cond_in['rms_weight']}

def reference(x, cond_1024, L0_cond_W_qkv, L0_cond_b_qkv, L0_cond_W_proj, L0_cond_b_proj, L0_cond_W_fc1, L0_cond_b_fc1, L0_cond_W_fc2, L0_cond_b_fc2, L0_cond_W_ada, L0_cond_b_ada, L1_cond_w_proj, L1_cond_b_proj, L1_cond_rms_weight):
    import jax
    import jax.numpy as jnp

    def _L0_cond_ref(x, c, W_qkv, b_qkv, W_proj, b_proj, W_fc1, b_fc1, W_fc2, b_fc2, W_ada, b_ada):
        import jax, jax.numpy as jnp
        import numpy as np
        HID = 256
        HEADS = 16
        HEAD_DIM = HID // HEADS
        MLP_HID = 1024
        TEMB = 256
        EPS = 1e-06

        def _ln(x):
            mu = jnp.mean(x, axis=-1, keepdims=True)
            var = jnp.var(x, axis=-1, keepdims=True)
            return (x - mu) * jax.lax.rsqrt(var + EPS)

        def _modulate(x, shift, scale):
            return x * (1.0 + scale[:, None, :]) + shift[:, None, :]

        def _attn(x, W_qkv, b_qkv, W_proj, b_proj):
            B, N, C = x.shape
            qkv = x @ W_qkv + b_qkv
            qkv = qkv.reshape(B, N, 3, HEADS, HEAD_DIM)
            q, k, v = (qkv[:, :, 0], qkv[:, :, 1], qkv[:, :, 2])
            scale = HEAD_DIM ** (-0.5)
            logits = jnp.einsum('bnhd,bmhd->bhnm', q, k) * scale
            attn = jax.nn.softmax(logits, axis=-1)
            out = jnp.einsum('bhnm,bmhd->bnhd', attn, v).reshape(B, N, C)
            return out @ W_proj + b_proj
        ada = jax.nn.silu(c) @ W_ada + b_ada
        shift_msa, scale_msa, gate_msa, shift_mlp, scale_mlp, gate_mlp = jnp.split(ada, 6, axis=1)
        h = _modulate(_ln(x), shift_msa, scale_msa)
        x = x + gate_msa[:, None, :] * _attn(h, W_qkv, b_qkv, W_proj, b_proj)
        h = _modulate(_ln(x), shift_mlp, scale_mlp)
        h = jax.nn.gelu(h @ W_fc1 + b_fc1, approximate=True) @ W_fc2 + b_fc2
        x = x + gate_mlp[:, None, :] * h
        return x

    def _L1_cond_ref(x, c, w_proj, b_proj, rms_weight):
        import jax, jax.numpy as jnp
        import numpy as np
        EPS_RMS = 1e-06
        EPS_Q = 1e-05

        def _weight_quant(w):
            scale = 1.0 / jnp.clip(jnp.mean(jnp.abs(w)), EPS_Q)
            wq = jnp.clip(jnp.round(w * scale), -1.0, 1.0) / scale
            return w + jax.lax.stop_gradient(wq - w)

        def _activation_quant(x):
            scale = 127.0 / jnp.clip(jnp.max(jnp.abs(x), axis=-1, keepdims=True), EPS_Q)
            xq = jnp.clip(jnp.round(x * scale), -128.0, 127.0) / scale
            return x + jax.lax.stop_gradient(xq - x)

        def _rmsnorm(x, weight):
            inv = jax.lax.rsqrt(jnp.mean(x * x, axis=-1, keepdims=True) + EPS_RMS)
            return x * inv * weight
        if c.ndim == 2:
            c = c[:, None, :]
        cq = _activation_quant(c)
        wq = _weight_quant(w_proj)
        emb = jnp.einsum('btc,dc->btd', cq, wq) + b_proj
        scale, shift = jnp.split(emb, 2, axis=-1)
        xn = _rmsnorm(x, rms_weight)
        return xn * (1.0 + scale) + shift
    x = _L0_cond_ref(x, cond_1024, L0_cond_W_qkv, L0_cond_b_qkv, L0_cond_W_proj, L0_cond_b_proj, L0_cond_W_fc1, L0_cond_b_fc1, L0_cond_W_fc2, L0_cond_b_fc2, L0_cond_W_ada, L0_cond_b_ada)
    x = _L1_cond_ref(x, cond_1024, L1_cond_w_proj, L1_cond_b_proj, L1_cond_rms_weight)
    return x

_drawn_inputs = setup_inputs


def setup_inputs(seed=0):
    import zlib

    import numpy as np

    out = dict(_drawn_inputs(seed))
    spreads = {'L0_cond_b_qkv': (0.0, 0.8),
     'L0_cond_b_proj': (0.0, 0.367),
     'L0_cond_b_fc1': (0.0, 0.8),
     'L0_cond_b_fc2': (0.0, 0.378),
     'L0_cond_b_ada': (0.0, 0.386),
     'L1_cond_b_proj': (0.0, 0.1),
     'L1_cond_rms_weight': (1.0, 0.2)}
    factors = {'L0_cond_W_qkv': 8.0, 'L0_cond_W_proj': 6.341}
    for name, (base, spread) in spreads.items():
        noise = np.random.default_rng([zlib.crc32(name.encode()), seed]).standard_normal(out[name].shape)
        drawn = base * np.exp(spread * noise) if base else spread * noise
        out[name] = jnp.asarray(drawn.astype(out[name].dtype))
    for name, factor in factors.items():
        out[name] = (out[name] * factor).astype(out[name].dtype)
    return out
```

```python
from contextlib import ExitStack

import concourse.bass as bass
from concourse import mybir

F32 = mybir.dt.float32
F32R = mybir.dt.float32r
BF16 = mybir.dt.bfloat16
ALU = mybir.AluOpType
ACT = mybir.ActivationFunctionType
AX = mybir.AxisListType

P = 128
BATCH, SEQ, D = 64, 64, 256
HEADS = 16
HD = D // HEADS
HID = 1024
TOK = 512
NB = TOK // SEQ
TILES = BATCH * SEQ // TOK
NS = TOK // P
KC = D // P
FC = HID // P
PAIRS = HEADS // 2
NI = PAIRS // KC
VW = HD + 1
NPR = 6
Q_RUNS, K_RUNS = ((0, 3, 0, 0), (3, 2, 1, 0), (5, 1, 2, 0)), ((0, 3, 0, 1), (3, 2, 0, 1), (5, 1, 0, 0))
ST = HD * NPR
LN_EPS, RMS_EPS, Q_EPS = 1e-6, 1e-6, 1e-5
ROUND = 1.5 * 2.0**23
SCALE = float(HD) ** -0.5


class Ring:

    def __init__(self, banks, filled, emptied, order, absent):
        self.banks, self.sem_filled, self.sem_emptied = banks, filled, emptied
        self.order, self.absent = order, absent

    def names(self, turn):
        return [n for n in self.order if not n.startswith(self.absent.get(turn, ()))]

    def per_bank(self, turn):
        return len(self.names(turn)) // len(self.banks)

    def place(self, name, turn):
        if isinstance(turn, int):
            k = self.names(turn).index(name)
            before = sum(self.per_bank(n) for n in range(-1, turn))
        else:
            k = self.order.index(name)
            first = self.per_bank(-1) + self.per_bank(0) - len(self.order) // len(self.banks)
            before = turn * (len(self.order) // len(self.banks)) + first
        return k % len(self.banks), before + k // len(self.banks)

    def bank(self, name, turn):
        return self.banks[self.place(name, turn)[0]]

    def free(self, name, turn):
        b, before = self.place(name, turn)
        return self.sem_emptied[b], before

    def filled(self, name, turn):
        b, before = self.place(name, turn)
        return self.sem_filled[b], before + 1

    def emptied(self, name, turn):
        b, before = self.place(name, turn)
        return self.sem_emptied[b], before + 1

    def signal_filled(self, name, turn):
        return self.sem_filled[self.place(name, turn)[0]], 1

    def signal_emptied(self, name, turn):
        return self.sem_emptied[self.place(name, turn)[0]], 1


def wait(eng, sem, value):
    if isinstance(value, int) and value <= 0:
        return
    eng.wait_ge(sem, value)


def row(ap, t):
    if isinstance(t, int):
        return ap[t]
    return ap[bass.ds(t, 1)].squeeze(0)


def build(nc, x, cT, c, w_qkv, bT_qkv, b_v, w_proj, b_proj, w_fc1, bT_fc1, w_fc2, b_fc2, w_ada, bT_ada,
          b_ada, w1T, b1, rms_w, ident, fold, select, out):
    with ExitStack() as ctx:
        def sb(name, shape, dt=F32):
            return ctx.enter_context(nc.sbuf_tensor(name, shape, dt))

        def sem(name):
            return ctx.enter_context(nc.semaphore(name))

        Wqkv = sb("Wqkv", [P, KC, 3 * D])
        Wp = sb("Wp", [P, KC, D])
        W1 = sb("W1", [P, KC, HID])
        W2 = sb("W2", [P, FC, D])
        bqk = sb("bqk", [P, 4])
        bqk_s = sb("bqk_s", [P, 4])
        b1T = sb("b1T", [P, FC])
        bv = sb("bv", [P, D])
        bp = sb("bp", [P, D])
        b2 = sb("b2", [P, D])
        idn = sb("idn", [P, P])
        fld = sb("fld", [P, SEQ])
        sel = sb("sel", [P, NI, P], F32R)
        halves = sb("halves", [P, NS])
        epss = sb("epss", [P, NS])
        waited = sb("waited", [P, 1])
        cTs = sb("cTs", [P, KC, BATCH])
        sil = sb("sil", [P, KC, BATCH])
        sg = sb("sg", [P, KC, BATCH])
        badaT = sb("badaT", [P, 8])
        bada = sb("bada", [BATCH, 2, D])
        cb = sb("cb", [BATCH, D])
        cq = sb("cq", [BATCH, D])
        cqT = sb("cqT", [P, KC, BATCH])
        cst = sb("cst", [BATCH, 4])
        wst = sb("wst", [P, 4])
        ones = sb("ones", [P, P])
        mod_all = sb("mod_all", [P, TILES, 8, NB])
        tok_vec = sb("tok_vec", [BATCH, 4, D])
        x_in = sb("x_in", [P, NS, D])
        x_res = sb("x_res", [P, NS, D])
        mod1 = sb("mod1", [P, 4, NB])
        gate1 = sb("gate1", [P, NS, D])
        st1 = sb("st1", [P, NS, 6])
        mv1 = sb("mv1", [P, NS, 2])
        ve1 = sb("ve1", [P, NS])
        rs1 = sb("rs1", [P, NS])
        hn = sb("hn", [P, NS, D])
        hS = sb("hS", [P, KC, TOK])
        hT1 = sb("hT1", [P, KC, TOK])
        qk32 = sb("qk32", [P, 2 * KC, TOK])
        qparts = sb("qparts", [P, KC, 3, TOK], BF16)
        kparts = sb("kparts", [P, KC, 3, TOK], BF16)
        qst = sb("qst", [P, HEADS, TOK], BF16)
        kst = sb("kst", [P, HEADS, TOK], BF16)
        rd = sb("rd", [P, TOK])
        v2 = sb("v2", [P, NB, PAIRS, 2, VW])
        nmax = sb("nmax", [P, KC, NI, NB])
        nmaxU = sb("nmaxU", [P, KC, NB, 2, NI, 2])
        nmaxT = sb("nmaxT", [P, KC, TOK], F32R)
        pT = sb("pT", [P, PAIRS, TOK])
        rden = sb("rden", [P, NS, HEADS])
        o = sb("o", [P, NS, D])
        oT = sb("oT", [P, KC, TOK])
        x1 = sb("x1", [P, NS, D])
        mod2 = sb("mod2", [P, 4, NB])
        vec2 = sb("vec2", [P, NS, 3, D])
        st2 = sb("st2", [P, NS, 6])
        mv2 = sb("mv2", [P, NS, 2])
        ve2 = sb("ve2", [P, NS])
        rs2 = sb("rs2", [P, NS])
        hT2 = sb("hT2", [P, KC, TOK])
        gT = sb("gT", [P, FC, TOK])
        xo = sb("xo", [P, NS, D])
        sq = sb("sq", [P, NS, D])
        ssq = sb("ssq", [P, NS])
        msq = sb("msq", [P, NS])
        rms = sb("rms", [P, NS])
        Wada = gT[:, 0:6, :].rearrange("p a b -> p (a b)").rearrange("p (k n) -> p k n", k=KC)
        Wc, Wcq = pT[:, 0:KC, :], pT[:, KC:2 * KC, :]
        sel32 = pT[:, 4, :].rearrange("p (i q) -> p i q", i=NI)
        emb, bc, rmsw = pT[0:BATCH, 5, :], pT[0:BATCH, 6, :], pT[0:BATCH, 7, 0:D]
        scr = nc.dram_tensor("scr", (BATCH, 4, D), F32, kind="Internal").ap()
        scr_qk = [[nc.dram_tensor(f"scr_{n}{c}", (P, NPR, TOK), BF16, kind="Internal").ap() for n in "qk"]
                  for c in range(KC)]
        lg = ctx.enter_context(nc.psum_tensor("lg", [P, NI, TOK], F32))
        gb = [ctx.enter_context(nc.psum_tensor(f"gb{i}", [P, TOK], F32)) for i in range(2)]
        tb = [ctx.enter_context(nc.psum_tensor(f"tb{i}", [P, TOK], F32)) for i in range(2)]

        fc1_names = [f"fc1_{j}" for j in range(FC)]
        gemm = Ring(gb, [sem(f"gemm_filled{i}") for i in range(2)], [sem(f"gemm_emptied{i}") for i in range(2)],
                    ["q0", "k0", "q1", "k1", "v0", "v1", *fc1_names, "fc2_0", "fc2_1", "proj0", "proj1"],
                    {-1: ("",), 0: ("fc",), TILES: ("q", "k", "v", "proj")})
        misc = Ring(tb, [sem(f"misc_filled{i}") for i in range(2)], [sem(f"misc_emptied{i}") for i in range(2)],
                    ["h2_0", "h2_1", "max0", "max1", "h1_0", "h1_1", "pv0", "pv1", "pv2", "pv3", "oT0", "oT1"],
                    {-1: ("h2", "max", "pv", "oT"), 0: ("h2",), TILES - 1: ("h1",),
                     TILES: ("max", "h1", "pv", "oT")})
        logit = Ring([lg], [sem("logits_filled")], [sem("logits_emptied")], ["s0", "s1", "sT0", "sT1"],
                     {-1: ("s",), TILES: ("s",)})

        consts_in = sem("consts_in")
        cond_in = sem("cond_in")
        weights_in = sem("weights_in")
        mlp_weights_in = sem("mlp_weights_in")
        prep = sem("prep")
        prep_act = sem("prep_act")
        prep_pe = sem("prep_pe")
        zeros_set = sem("zeros_set")
        scratch_out = sem("scratch_out")
        x_in_ready = sem("x_in_ready")
        mod1_in = sem("mod1_in")
        gate1_in = sem("gate1_in")
        mod2_in = sem("mod2_in")
        vec2_in = sem("vec2_in")
        x_res_ready = sem("x_res_ready")
        ln1_step = sem("ln1_step")
        ln1_rstd = sem("ln1_rstd")
        hn1_ready = sem("hn1_ready")
        hT1_ready = sem("hT1_ready")
        parts_step = sem("parts_step")
        parts_ready = sem("parts_ready")
        parts_out = [sem(f"parts_out_{n}{c}") for c in range(KC) for n in "qk"]
        stacks_in = [sem(f"stacks_in{c}") for c in range(KC)]
        nmax_step = sem("nmax_step")
        nmaxU_ready = sem("nmaxU_ready")
        rden_ready = sem("rden_ready")
        attn_gated = sem("attn_gated")
        x1_ready = sem("x1_ready")
        ln2_step = sem("ln2_step")
        ln2_rstd = sem("ln2_rstd")
        hn2_ready = sem("hn2_ready")
        hT2_ready = sem("hT2_ready")
        mlp_gated = sem("mlp_gated")
        x2_ready = sem("x2_ready")
        ssq_ready = sem("ssq_ready")
        msq_ready = sem("msq_ready")
        rms_ready = sem("rms_ready")
        ys_ready = sem("ys_ready")
        y_ready = sem("y_ready")
        y_stored = [sem(f"y_stored{k}") for k in range(2)]

        block = ctx.enter_context(nc.Block())

        def turns(eng, body):
            body(0, attn=True, mlp=False, late=False, more=True)
            body(1, attn=True, mlp=True, late=False, more=True)
            with eng.Fori(2, TILES - 1) as t:
                body(t, attn=True, mlp=True, late=True, more=True)
            body(TILES - 1, attn=True, mlp=True, late=True, more=False)
            body(TILES, attn=False, mlp=True, late=True, more=False)
            body(TILES + 1, attn=False, mlp=False, late=True, more=False)

        x_v = x.rearrange("(t s p) f -> t p s f", s=NS, p=P)
        out_v = out.rearrange("(t s p) f -> t p s f", s=NS, p=P)
        scr_v = scr.rearrange("(t s h) v f -> t h s v f", s=NS, h=2)

        def mods(t, v):
            if isinstance(t, int):
                return mod_all[:, t, v:v + 4, :]
            return mod_all[:, bass.ds(t, 1), v:v + 4, :].squeeze(1)

        @block.sync
        def _(sp):
            for dst, src in ((cTs, cT), (cb, c), (Wada, w_ada), (Wc, w1T), (badaT, bT_ada)):
                sp.dma_start(dst[:], src).then_inc(cond_in, 16)
            for k, g in enumerate((2, 5)):
                sp.dma_start(bada[:, k, :], b_ada[:, g * D:(g + 1) * D].partition_broadcast(BATCH).rearrange(
                    "p a f -> p (a f)")).then_inc(cond_in, 16)
            sp.dma_start(bc[:], b1.partition_broadcast(BATCH).rearrange("p a f -> p (a f)")).then_inc(cond_in, 16)
            sp.dma_start(rmsw[:], rms_w.partition_broadcast(BATCH).rearrange("p a f -> p (a f)")).then_inc(cond_in, 16)
            sp.dma_start(x_in[:], x_v[0]).then_inc(x_in_ready, 16)
            for dst, src in ((idn, ident), (fld, fold), (sel32, select), (bqk, bT_qkv), (b1T, bT_fc1)):
                sp.dma_start(dst[:], src).then_inc(consts_in, 16)
            for dst, src in ((bv, b_v), (bp, b_proj), (b2, b_fc2)):
                sp.dma_start(dst[:], src.partition_broadcast(P).rearrange("p a f -> p (a f)")).then_inc(consts_in, 16)
            sp.dma_start(Wqkv[:], w_qkv).then_inc(weights_in, 16)
            sp.dma_start(Wp[:], w_proj).then_inc(weights_in, 16)
            sp.dma_start(W1[:], w_fc1).then_inc(mlp_weights_in, 16)
            sp.dma_start(W2[:], w_fc2).then_inc(mlp_weights_in, 16)
            sp.wait_ge(prep, PREP_TOK)
            sp.dma_start(scr, tok_vec[:]).then_inc(scratch_out, 16)
            sp.dma_start(mod1[:], mod_all[:, 0, 0:4, :]).then_inc(mod1_in, 16)
            sp.wait_ge(scratch_out, 16)
            for h in range(2):
                sp.dma_start(gate1[h * SEQ:(h + 1) * SEQ, :, :], scr_v[0, h, :, 0, :].partition_broadcast(SEQ)
                             ).then_inc(gate1_in, 16)

            def store(tile, k):
                sp.wait_ge(y_ready, tile * 2 + k + 1)
                sp.dma_start(row(out_v, tile)[:, 2 * k:2 * k + 2, :], xo[:, 2 * k:2 * k + 2, :]
                             ).then_inc(y_stored[k], 16)

            def body(t, attn, mlp, late, more):
                u, w = t - 1, t - 2
                if mlp:
                    wait(sp, hT2_ready, u * KC)
                    sp.dma_start(mod2[:], mods(u, 4)).then_inc(mod2_in, 16)
                if attn:
                    if not (isinstance(t, int) and t == 0):
                        sp.wait_ge(*logit.filled("sT1", u))
                    for c in range(KC):
                        for n, (parts, runs) in enumerate(((qparts, Q_RUNS), (kparts, K_RUNS))):
                            sp.wait_ge(parts_ready, t * 4 + 2 * c + n + 1)
                            for first, rows, part, step in runs:
                                src = parts[:, c, part:part + (rows if step else 1), :]
                                if rows > 1 and not step:
                                    src = src.broadcast_to([P, rows, TOK])
                                sp.dma_start(scr_qk[c][n][:, first:first + rows, :], src
                                             ).then_inc(parts_out[2 * c + n], 16)
                        for n, stack in enumerate((qst, kst)):
                            sp.wait_ge(parts_out[2 * c + n], (t + 1) * 16 * len(Q_RUNS))
                            sp.dma_start(stack[0:ST, c * HEADS // KC:(c + 1) * HEADS // KC, :],
                                         scr_qk[c][n].rearrange("(h d) a t -> (d a) h t", d=HD)
                                         ).then_inc(stacks_in[c], 16)
                if late:
                    store(w, 1)
                if more:
                    sp.wait_ge(hn1_ready, (t + 1) * NS)
                    sp.wait_ge(x_res_ready, t + 1)
                    sp.dma_start(x_in[:], row(x_v, t + 1)).then_inc(x_in_ready, 16)
                    sp.wait_ge(hT1_ready, (t + 1) * KC)
                    sp.dma_start(mod1[:], mods(t + 1, 0)).then_inc(mod1_in, 16)
                if mlp:
                    wait(sp, y_ready, u * 2)
                    for h in range(2):
                        sp.dma_start(vec2[h * SEQ:(h + 1) * SEQ, :, :, :],
                                     row(scr_v, u)[h, :, 1:4, :].partition_broadcast(SEQ)).then_inc(vec2_in, 16)
                    store(u, 0)
                if more:
                    sp.wait_ge(attn_gated, (t + 1) * 2)
                    for h in range(2):
                        sp.dma_start(gate1[h * SEQ:(h + 1) * SEQ, :, :],
                                     row(scr_v, t + 1)[h, :, 0, :].partition_broadcast(SEQ)).then_inc(gate1_in, 16)

            turns(sp, body)
            sp.wait_ge(y_stored[0], 16 * TILES)
            sp.wait_ge(y_stored[1], 16 * TILES)

        @block.tensor
        def _(pe):
            mm = nc.tensor.matmul
            pe.wait_ge(prep, PREP_WABS)
            mm(tb[1][:, 0:2], ones[:], wst[:, 0:2], start=True, stop=True).then_inc(prep_pe, 1)
            pe.wait_ge(prep, PREP_SILU)
            pe.wait_ge(cond_in, COND_ALL)
            for n, col in enumerate(MOD_COLS):
                for k in range(KC):
                    last = mm(gb[0][:, n * BATCH:(n + 1) * BATCH], Wada[:, k, col:col + P], sil[:, k, :],
                              start=(k == 0), stop=(k == KC - 1))
            last.then_inc(prep_pe, 1)
            for n, g in enumerate((2, 5)):
                for k in range(KC):
                    last = mm(gb[1][0:BATCH, n * D:(n + 1) * D], sil[:, k, :], Wada[:, k, g * D:(g + 1) * D],
                              start=(k == 0), stop=(k == KC - 1))
            last.then_inc(prep_pe, 1)
            pe.wait_ge(prep, PREP_CQ)
            pe.wait_ge(consts_in, CONSTS_ALL)
            for k in range(KC):
                last = nc.tensor.transpose(tb[0][:, k * BATCH:(k + 1) * BATCH], cq[:, k * P:(k + 1) * P],
                                           idn[0:BATCH, 0:BATCH])
            last.then_inc(prep_pe, 1)
            pe.wait_ge(prep, PREP_CQT)
            for k in range(KC):
                last = mm(lg[0:BATCH, 0, :], cqT[:, k, :], Wcq[:, k, :], start=(k == 0), stop=(k == KC - 1))
            last.then_inc(prep_pe, 1)
            pe.wait_ge(prep, PREP_ALL)
            pe.wait_ge(weights_in, 32)
            pe.wait_ge(zeros_set, ZEROS_ALL)

            def to_features(name, t, src):
                c = int(name[-1])
                wait(pe, *misc.free(name, t))
                for s in range(NS):
                    last = nc.tensor.transpose(misc.bank(name, t)[:, s * P:(s + 1) * P],
                                               src[:, s, c * P:(c + 1) * P], idn[:])
                last.then_inc(*misc.signal_filled(name, t))

            def fc1(names, t, u):
                for n in names:
                    j = int(n[4:])
                    wait(pe, *gemm.free(n, t))
                    for k in range(KC):
                        last = mm(gemm.bank(n, t)[:], W1[:, k, j * P:(j + 1) * P], hT2[:, k, :],
                                  start=(k == 0), stop=(k == KC - 1))
                    last.then_inc(*gemm.signal_filled(n, t))

            def rows_out(name, t, src, w, chunks):
                h = int(name[-1])
                wait(pe, *gemm.free(name, t))
                for s in range(2):
                    tok = (2 * h + s) * P
                    for k in range(chunks):
                        last = mm(gemm.bank(name, t)[:, s * D:(s + 1) * D], src[:, k, tok:tok + P], w[:, k, :],
                                  start=(k == 0), stop=(k == chunks - 1))
                last.then_inc(*gemm.signal_filled(name, t))

            def logits(name, t):
                c = int(name[-1])
                st = name.startswith("sT")
                wait(pe, *logit.free(name, t))
                if st:
                    pe.wait_ge(*misc.emptied(f"max{c}", t))
                    for i in range(NI):
                        mm(lg[:, i, :], sel[:, i, :], nmaxT[:, c, :], start=True, stop=False, skip_group_check=True)
                stat, mov = (kst, qst) if st else (qst, kst)
                for j in range(2):
                    for b in range(NB):
                        tk = slice(b * SEQ, (b + 1) * SEQ)
                        for i in range(NI):
                            head = 2 * (c * NI + i) + j
                            last = mm(lg[j * SEQ:(j + 1) * SEQ, i, tk], stat[0:ST, head, tk], mov[0:ST, head, tk],
                                      start=(not st), stop=True, skip_group_check=True)
                last.then_inc(*logit.signal_filled(name, t))

            def turn_max(c, t):
                n = f"max{c}"
                pe.wait_ge(nmaxU_ready, t * KC + c + 1)
                wait(pe, *misc.free(n, t))
                for b in range(NB):
                    last = mm(misc.bank(n, t)[0:4 * NI, b * SEQ:(b + 1) * SEQ],
                              nmaxU[:, c, b, :, :, :].rearrange("p a i j -> p (a i j)"), fld[:],
                              start=True, stop=True)
                last.then_inc(*misc.signal_filled(n, t))

            def rows_of_next(turn):
                pe.wait_ge(hn1_ready, (turn + 2) * NS)
                to_features("h1_0", turn, hn)
                to_features("h1_1", turn, hn)

            rows_of_next(-1)

            def body(t, attn, mlp, late, more):
                u = t - 1
                if attn:
                    pe.wait_ge(hT1_ready, (t + 1) * KC)
                    for n in ("q0", "k0", "q1", "k1"):
                        col = (D if n[0] == "k" else 0) + int(n[1]) * P
                        wait(pe, *gemm.free(n, t))
                        for k in range(KC):
                            last = mm(gemm.bank(n, t)[:], Wqkv[:, k, col:col + P], hT1[:, k, :],
                                      start=(k == 0), stop=(k == KC - 1))
                        last.then_inc(*gemm.signal_filled(n, t))
                    rows_out("v0", t, hT1, Wqkv[:, :, 2 * D:3 * D], KC)
                    rows_out("v1", t, hT1, Wqkv[:, :, 2 * D:3 * D], KC)
                if mlp:
                    pe.wait_ge(hn2_ready, (u + 1) * NS)
                    to_features("h2_0", t, hn)
                    to_features("h2_1", t, hn)
                if attn:
                    pe.wait_ge(stacks_in[0], (t + 1) * STACK_LOADS)
                    logits("s0", t)
                if mlp:
                    pe.wait_ge(mlp_weights_in, 32)
                    pe.wait_ge(hT2_ready, (u + 1) * KC)
                    fc1(fc1_names[0:3], t, u)
                if attn:
                    pe.wait_ge(stacks_in[1], (t + 1) * STACK_LOADS)
                    logits("s1", t)
                    turn_max(0, t)
                if mlp:
                    fc1(fc1_names[3:5], t, u)
                if attn:
                    turn_max(1, t)
                    logits("sT0", t)
                if mlp:
                    fc1(fc1_names[5:7], t, u)
                if attn:
                    logits("sT1", t)
                if more:
                    rows_of_next(t)
                if mlp:
                    fc1(fc1_names[7:8], t, u)
                if attn:
                    pe.wait_ge(*logit.emptied("sT1", t))
                    pe.wait_ge(*gemm.emptied("v0", t))
                    pe.wait_ge(*gemm.emptied("v1", t))
                    for n in ("pv0", "pv1", "pv2", "pv3"):
                        wait(pe, *misc.free(n, t))
                        for bb in range(2):
                            b = 2 * int(n[2]) + bb
                            for p in range(PAIRS):
                                last = mm(misc.bank(n, t)[bb * SEQ:(bb + 1) * SEQ, p * 2 * VW:(p + 1) * 2 * VW],
                                          pT[:, p, b * SEQ:(b + 1) * SEQ],
                                          v2[:, b, p, :, :].rearrange("p j e -> p (j e)"), start=True, stop=True)
                        last.then_inc(*misc.signal_filled(n, t))
                    pe.wait_ge(*misc.emptied("pv2", t))
                    pe.wait_ge(*misc.emptied("pv3", t))
                    to_features("oT0", t, o)
                    to_features("oT1", t, o)
                if mlp:
                    pe.wait_ge(*gemm.emptied(f"fc1_{FC - 2}", t))
                    pe.wait_ge(*gemm.emptied(f"fc1_{FC - 1}", t))
                    rows_out("fc2_0", t, gT, W2, FC)
                    rows_out("fc2_1", t, gT, W2, FC)
                if attn:
                    pe.wait_ge(*misc.emptied("oT0", t))
                    pe.wait_ge(*misc.emptied("oT1", t))
                    rows_out("proj0", t, oT, Wp, KC)
                    rows_out("proj1", t, oT, Wp, KC)

            turns(pe, body)

        @block.scalar
        def _(act):
            act.wait_ge(cond_in, COND_ALL)
            nc.scalar.activation(sg[:], cTs[:], ACT.Exp, scale=-1.0).then_inc(prep_act, 1)
            act.wait_ge(consts_in, CONSTS_ALL)
            nc.scalar.mul(bqk_s[:], bqk[:], SCALE).then_inc(prep_act, 1)
            act.wait_ge(prep_act, 2)

            def squares(tile, k):
                act.wait_ge(x2_ready, tile * 2 + k + 1)
                for s in (2 * k, 2 * k + 1):
                    nc.scalar.activation(sq[:, s, :], xo[:, s, :], ACT.Square, scale=float(D) ** -0.5,
                                         accum_out=ssq[:, s:s + 1]).then_inc(ssq_ready, 1)

            def body(t, attn, mlp, late, more):
                u, w = t - 1, t - 2

                def queries_keys(n):
                    c = int(n[1])
                    act.wait_ge(*gemm.filled(n, t))
                    if n[0] == "q":
                        ins = nc.scalar.activation(qk32[:, c, :], gemm.bank(n, t)[:], ACT.Identity,
                                                   bias=bqk_s[:, c:c + 1], scale=SCALE)
                    else:
                        ins = nc.scalar.activation(qk32[:, KC + c, :], gemm.bank(n, t)[:], ACT.Identity,
                                                   bias=bqk[:, KC + c:KC + c + 1])
                    ins.then_inc(*gemm.signal_emptied(n, t))

                def max_rows(c):
                    act.wait_ge(*misc.filled(f"max{c}", t))
                    nc.scalar.copy(nmaxT[0:4 * NI, c, :], misc.bank(f"max{c}", t)[0:4 * NI, :]
                                   ).then_inc(*misc.signal_emptied(f"max{c}", t))

                def probabilities(c):
                    act.wait_ge(*logit.filled(f"sT{c}", t))
                    if c == 0 and not (isinstance(t, int) and t == 0):
                        act.wait_ge(*misc.filled("pv2", u))
                        act.wait_ge(*misc.filled("pv3", u))
                    nc.scalar.activation(pT[:, c * NI:(c + 1) * NI, :], lg[:], ACT.Exp
                                         ).then_inc(*logit.signal_emptied(f"sT{c}", t))

                def gelu(names):
                    for n in names:
                        j = int(n[4:])
                        act.wait_ge(*gemm.filled(n, t))
                        nc.scalar.activation(gT[:, j, :], gemm.bank(n, t)[:], ACT.Gelu_apprx_tanh,
                                             bias=b1T[:, j:j + 1]).then_inc(*gemm.signal_emptied(n, t))

                if attn:
                    wait(act, x1_ready, t * 2)
                    act.wait_ge(x_in_ready, (t + 1) * 16)
                    nc.scalar.copy(x_res[:], x_in[:]).then_inc(x_res_ready, 1)
                    wait(act, parts_ready, t * 4)
                    queries_keys("q0")
                    queries_keys("k0")
                if late:
                    squares(w, 1)
                if attn:
                    queries_keys("q1")
                    queries_keys("k1")
                if mlp:
                    gelu(fc1_names[0:3])
                if attn:
                    max_rows(0)
                if mlp:
                    gelu(fc1_names[3:5])
                if attn:
                    max_rows(1)
                    probabilities(0)
                if mlp:
                    gelu(fc1_names[5:7])
                if attn:
                    probabilities(1)
                if mlp:
                    gelu(fc1_names[7:8])
                if attn:
                    for c in range(KC):
                        act.wait_ge(*misc.filled(f"oT{c}", t))
                        if c == 0 and not (isinstance(t, int) and t == 0):
                            act.wait_ge(*gemm.filled("proj0", u))
                            act.wait_ge(*gemm.filled("proj1", u))
                        nc.scalar.copy(oT[:, c, :], misc.bank(f"oT{c}", t)[:]
                                       ).then_inc(*misc.signal_emptied(f"oT{c}", t))
                if mlp:
                    squares(u, 0)

            turns(act, body)

        @block.vector
        def _(dve):
            v = nc.vector
            steps = [0]

            def link(ins):
                steps[0] += 1
                ins.then_inc(prep, 1)
                dve.wait_ge(prep, steps[0])

            v.memset(v2[:], 0.0).then_inc(zeros_set, 1)
            v.memset(nmaxU[:], 0.0).then_inc(zeros_set, 1)
            v.memset(nmaxT[:].bitcast(F32), 0.0).then_inc(zeros_set, 1)
            v.memset(halves[:], -0.5).then_inc(zeros_set, 1)
            v.memset(epss[:], RMS_EPS).then_inc(zeros_set, 1)
            dve.wait_ge(zeros_set, 5)
            v.memset(v2[0:SEQ, :, :, 0, HD:VW], 1.0).then_inc(zeros_set, 1)
            v.memset(v2[SEQ:P, :, :, 1, HD:VW], 1.0).then_inc(zeros_set, 1)
            link(v.memset(wst[:], 0.0))
            link(v.memset(ones[:], 1.0))
            dve.wait_ge(cond_in, COND_ALL)
            link(v.tensor_reduce(wst[:, 0:1], Wc[:].rearrange("p k n -> p (k n)"), AX.X, ALU.add,
                                 apply_absolute_value=True))
            assert steps[0] == PREP_WABS
            dve.wait_ge(prep_act, 1)
            link(v.tensor_scalar(sil[:], sg[:], 1.0, None, ALU.add))
            link(v.reciprocal(sg[:], sil[:]))
            link(v.tensor_tensor(sil[:], cTs[:], sg[:], ALU.mult))
            assert steps[0] == PREP_SILU
            link(v.tensor_reduce(cst[:, 0:1], cb[:], AX.X, ALU.max, apply_absolute_value=True))
            link(v.tensor_scalar(cst[:, 0:1], cst[:, 0:1], Q_EPS, None, ALU.max))
            link(v.reciprocal(cst[:, 1:2], cst[:, 0:1]))
            link(v.tensor_scalar(cst[:, 1:2], cst[:, 1:2], 127.0, None, ALU.mult))
            link(v.tensor_scalar(cq[:], cb[:], cst[:, 1:2], ROUND, ALU.mult, ALU.add))
            link(v.tensor_scalar(cq[:], cq[:], ROUND, 127.0, ALU.subtract, ALU.min))
            link(v.tensor_scalar(cq[:], cq[:], -128.0, None, ALU.max))
            assert steps[0] == PREP_CQ
            dve.wait_ge(prep_pe, 1)
            link(v.tensor_scalar(wst[:, 2:3], tb[1][:, 0:1], 1.0 / (2 * D * D), Q_EPS, ALU.mult, ALU.max))
            link(v.reciprocal(wst[:, 3:4], wst[:, 2:3]))
            link(v.tensor_scalar(Wcq[:], Wc[:], wst[:, 3:4], ROUND, ALU.mult, ALU.add))
            link(v.tensor_scalar(Wcq[:], Wcq[:], ROUND, 1.0, ALU.subtract, ALU.min))
            link(v.tensor_scalar(Wcq[:], Wcq[:], -1.0, None, ALU.max))
            dve.wait_ge(prep_pe, 4)
            link(v.tensor_copy(cqT[:].rearrange("p k b -> p (k b)"), tb[0][:, 0:KC * BATCH]))
            assert steps[0] == PREP_CQT
            link(v.tensor_tensor(mod_all[:].rearrange("p t v b -> p v t b"),
                                 gb[0][:].rearrange("p (v t b) -> p v t b", v=8, t=TILES),
                                 badaT[:].unsqueeze(2).unsqueeze(3).broadcast_to([P, 8, TILES, NB]), ALU.add))
            scales = mod_all[:].rearrange("p t (w z) b -> p w t (z b)", w=4)
            for w in (1, 3):
                link(v.tensor_scalar(scales[:, w, :, :], scales[:, w, :, :], 1.0, None, ALU.add))
            link(v.tensor_tensor(tok_vec[:, 0:2, :], gb[1][0:BATCH, :].rearrange("p (v f) -> p v f", v=2), bada[:],
                                 ALU.add))
            link(v.tensor_scalar(cst[:, 2:3], cst[:, 0:1], 1.0 / 127.0, wst[0:BATCH, 2:3], ALU.mult, ALU.mult))
            dve.wait_ge(prep_pe, 5)
            link(v.scalar_tensor_tensor(emb[:], lg[0:BATCH, 0, :], cst[:, 2:3], bc[:], ALU.mult, ALU.add))
            link(v.scalar_tensor_tensor(tok_vec[:, 2, :], emb[:, 0:D], 1.0, rmsw[:], ALU.add, ALU.mult))
            link(v.tensor_copy(tok_vec[:, 3, :], emb[:, D:2 * D]))
            assert steps[0] == PREP_TOK
            dve.wait_ge(consts_in, CONSTS_ALL)
            link(v.tensor_copy(sel[:], sel32[:]))
            assert steps[0] == PREP_ALL

            def normalise(t, src, st, mv, ve, rs, dst, step, rstd, ready, eps):
                base = t * 3
                for s in range(NS):
                    last = v.bn_stats(st[:, s, :], src[:, s, :])
                last.then_inc(step, 1)
                dve.wait_ge(step, base + 1)
                v.memset(waited[:], 0.0)
                for s in range(NS):
                    last = v.bn_aggr(mv[:, s, :], st[:, s, :])
                last.then_inc(step, 1)
                dve.wait_ge(step, base + 2)
                v.tensor_scalar(ve[:], mv[:, :, 1], eps, None, ALU.add).then_inc(step, 1)
                dve.wait_ge(rstd, t + 1)
                for s in range(NS):
                    v.tensor_scalar(dst[:, s, :], src[:, s, :], mv[:, s, 0:1], rs[:, s:s + 1], ALU.subtract, ALU.mult
                                    ).then_inc(ready, 1)

            def scale_columns(name, t, mod, dst):
                c = int(name[-1])
                dve.wait_ge(*misc.filled(name, t))
                v.tensor_tensor(dst[:, c, :].rearrange("p (b n) -> p b n", b=NB),
                                misc.bank(name, t)[:].rearrange("p (b n) -> p b n", b=NB),
                                mod[:, KC + c, :].unsqueeze(2).broadcast_to([P, NB, SEQ]), ALU.mult
                                ).then_inc(*misc.signal_emptied(name, t))

            def rows_in(name, t, bias, dst):
                h = int(name[-1])
                dve.wait_ge(*gemm.filled(name, t))
                v.tensor_tensor(dst[:, 2 * h:2 * h + 2, :], gemm.bank(name, t)[:].rearrange("p (s f) -> p s f", s=2),
                                bias[:].unsqueeze(1).broadcast_to([P, 2, D]), ALU.add
                                ).then_inc(*gemm.signal_emptied(name, t))

            def ln1(t):
                dve.wait_ge(x_in_ready, (t + 1) * 16)
                normalise(t, x_in, st1, mv1, ve1, rs1, hn, ln1_step, ln1_rstd, hn1_ready, LN_EPS)

            def columns_of_next(turn):
                dve.wait_ge(mod1_in, (turn + 2) * 16)
                wait(dve, hT2_ready, turn * KC)
                scale_columns("h1_0", turn, mod1, hS)
                scale_columns("h1_1", turn, mod1, hS)

            dve.wait_ge(scratch_out, 16)
            ln1(0)
            columns_of_next(-1)

            def body(t, attn, mlp, late, more):
                u, w = t - 1, t - 2

                def split(n):
                    c = int(n[1])
                    src = qk32[:, (KC if n[0] == "k" else 0) + c, :]
                    dst = (kparts if n[0] == "k" else qparts)[:, c, :, :]
                    done = t * 16 + 4 * ("q0", "k0", "q1", "k1").index(n)
                    dve.wait_ge(*gemm.emptied(n, t))
                    wait(dve, stacks_in[c], t * STACK_LOADS)
                    v.tensor_copy(dst[:, 0, :], src).then_inc(parts_step, 1)
                    dve.wait_ge(parts_step, done + 1)
                    v.tensor_tensor(rd[:], src, dst[:, 0, :], ALU.subtract).then_inc(parts_step, 1)
                    dve.wait_ge(parts_step, done + 2)
                    v.tensor_copy(dst[:, 1, :], rd[:]).then_inc(parts_step, 1)
                    dve.wait_ge(parts_step, done + 3)
                    v.tensor_tensor(dst[:, 2, :], rd[:], dst[:, 1, :], ALU.subtract).then_inc(parts_step, 1)
                    dve.wait_ge(parts_step, done + 4)
                    v.memset(waited[:], 0.0).then_inc(parts_ready, 1)

                def maxima(c):
                    dve.wait_ge(*logit.filled(f"s{c}", t))
                    v.tensor_reduce(nmax[:, c, :, :], lg[:].rearrange("p i (b m) -> p i b m", b=NB), AX.X, ALU.max,
                                    negate=True).then_inc(*logit.signal_emptied(f"s{c}", t))
                    dve.wait_ge(*logit.emptied(f"s{c}", t))
                    halves_of = ((0, slice(0, SEQ)), (1, slice(SEQ, P)))
                    for j, r in halves_of:
                        v.tensor_copy(nmaxU[r, c, :, 0, :, j].bitcast(F32R),
                                      nmax[r, c, :, :].rearrange("p i b -> p b i")).then_inc(nmax_step, 1)
                    dve.wait_ge(nmax_step, t * 4 + 2 * c + 2)
                    for j, r in halves_of:
                        last = v.tensor_tensor(nmaxU[r, c, :, 1, :, j], nmax[r, c, :, :].rearrange("p i b -> p b i"),
                                               nmaxU[r, c, :, 0, :, j], ALU.subtract)
                    last.then_inc(nmaxU_ready, 1)

                def scale_rows(tile, k):
                    dve.wait_ge(rms_ready, tile * 2 + k + 1)
                    for s in (2 * k, 2 * k + 1):
                        last = v.scalar_tensor_tensor(xo[:, s, :], xo[:, s, :], rms[:, s:s + 1], vec2[:, s, 1, :],
                                                      ALU.mult, ALU.mult)
                    last.then_inc(ys_ready, 1)

                if attn:
                    for n in ("q0", "k0", "q1", "k1"):
                        split(n)
                    if not (isinstance(t, int) and t == 0):
                        dve.wait_ge(*misc.filled("pv2", u))
                        dve.wait_ge(*misc.filled("pv3", u))
                    for n in ("v0", "v1"):
                        dve.wait_ge(*gemm.filled(n, t))
                        halves_of = ((0, slice(0, SEQ)), (1, slice(SEQ, P)))
                        for h, r in halves_of:
                            for j, to in halves_of:
                                last = v.tensor_tensor(
                                    v2[to, :, :, j, 0:HD].rearrange("p (a h) q d -> p a h q d", h=2)[
                                        :, 2 * int(n[1]):2 * int(n[1]) + 2, h, :, :],
                                    gemm.bank(n, t)[r, :].rearrange("p (a q j d) -> p a q j d", a=2, j=2, d=HD)[
                                        :, :, :, j, :],
                                    bv[r, :].rearrange("p (q j d) -> p q j d", j=2, d=HD)[:, :, j, :].unsqueeze(1)
                                    .broadcast_to([SEQ, 2, PAIRS, HD]), ALU.add)
                        last.then_inc(*gemm.signal_emptied(n, t))
                if late:
                    scale_rows(w, 1)
                if mlp:
                    dve.wait_ge(mod2_in, (u + 1) * 16)
                    if attn:
                        dve.wait_ge(hT1_ready, (t + 1) * KC)
                    scale_columns("h2_0", t, mod2, hS)
                    scale_columns("h2_1", t, mod2, hS)
                if attn:
                    maxima(0)
                    maxima(1)
                if more:
                    ln1(t + 1)
                    columns_of_next(t)
                if attn:
                    for k, n in enumerate(("pv0", "pv1", "pv2", "pv3")):
                        heads = misc.bank(n, t)[:, 0:HEADS * VW].rearrange("p (h e) -> p h e", e=VW)
                        dve.wait_ge(*misc.filled(n, t))
                        v.reciprocal(rden[:, k, :], heads[:, :, HD]).then_inc(rden_ready, 1)
                        if k == 0:
                            wait(dve, x1_ready, t * 2)
                        dve.wait_ge(rden_ready, t * NS + k + 1)
                        v.tensor_tensor(o[:, k, :].rearrange("p (h d) -> p h d", d=HD), heads[:, :, 0:HD],
                                        rden[:, k, :].unsqueeze(2).broadcast_to([P, HEADS, HD]), ALU.mult
                                        ).then_inc(*misc.signal_emptied(n, t))
                if mlp:
                    wait(dve, y_stored[0], u * 16)
                    rows_in("fc2_0", t, b2, xo)
                    wait(dve, y_stored[1], u * 16)
                    rows_in("fc2_1", t, b2, xo)
                    scale_rows(u, 0)
                if attn:
                    dve.wait_ge(*misc.filled("oT0", t))
                    dve.wait_ge(*misc.filled("oT1", t))
                    rows_in("proj0", t, bp, o)
                    rows_in("proj1", t, bp, o)
                    dve.wait_ge(x1_ready, (t + 1) * 2)
                    normalise(t, x1, st2, mv2, ve2, rs2, hn, ln2_step, ln2_rstd, hn2_ready, LN_EPS)

            turns(dve, body)

        @block.gpsimd
        def _(pool):
            g = nc.gpsimd

            def power(src, dst, ready):
                g.tensor_tensor(dst, src, halves[:, 0:src.shape[1]], ALU.pow).then_inc(ready, 1)

            def shift_columns(t, mod, mod_in, src, dst, stage, turn, ready):
                pool.wait_ge(mod_in, (t + 1) * 16)
                for c in range(KC):
                    pool.wait_ge(*misc.emptied(f"{stage}_{c}", turn))
                    g.tensor_tensor(dst[:, c, :].rearrange("p (b n) -> p b n", b=NB),
                                    src[:, c, :].rearrange("p (b n) -> p b n", b=NB),
                                    mod[:, c, :].unsqueeze(2).broadcast_to([P, NB, SEQ]), ALU.add).then_inc(ready, 1)

            def gate_and_add(k, t, name, turn, acc, gate, gated, res, dst, ready):
                s = slice(2 * k, 2 * k + 2)
                pool.wait_ge(*gemm.emptied(name, turn))
                g.tensor_tensor(acc[:, s, :], acc[:, s, :], gate[:, s, :], ALU.mult).then_inc(gated, 1)
                pool.wait_ge(gated, t * 2 + k + 1)
                g.tensor_tensor(dst[:, s, :], res[:, s, :], acc[:, s, :], ALU.add).then_inc(ready, 1)

            def next_columns(turn):
                pool.wait_ge(ln1_step, (turn + 2) * 3)
                power(ve1[:], rs1[:], ln1_rstd)
                if not (isinstance(turn, int) and turn < 0):
                    pool.wait_ge(*gemm.filled("v0", turn))
                    pool.wait_ge(*gemm.filled("v1", turn))
                shift_columns(turn + 1, mod1, mod1_in, hS, hT1, "h1", turn, hT1_ready)

            pool.wait_ge(zeros_set, ZEROS_ALL)
            next_columns(-1)

            def body(t, attn, mlp, late, more):
                u, w = t - 1, t - 2

                def mean_square(tile, k):
                    s = slice(2 * k, 2 * k + 2)
                    pool.wait_ge(ssq_ready, tile * NS + 2 * k + 2)
                    g.tensor_tensor(msq[:, s], ssq[:, s], epss[:, s], ALU.add).then_inc(msq_ready, 1)
                    pool.wait_ge(msq_ready, tile * 2 + k + 1)
                    power(msq[:, s], rms[:, s], rms_ready)

                def shift_rows(tile, k):
                    s = slice(2 * k, 2 * k + 2)
                    pool.wait_ge(ys_ready, tile * 2 + k + 1)
                    g.tensor_tensor(xo[:, s, :], xo[:, s, :], vec2[:, s, 2, :], ALU.add).then_inc(y_ready, 1)

                if late:
                    mean_square(w, 1)
                    shift_rows(w, 1)
                if mlp:
                    shift_columns(u, mod2, mod2_in, hS, hT2, "h2", t, hT2_ready)
                if more:
                    next_columns(t)
                if mlp:
                    pool.wait_ge(vec2_in, (u + 1) * 32)
                    gate_and_add(0, u, "fc2_0", t, xo, vec2[:, :, 0, :], mlp_gated, x1, xo, x2_ready)
                    mean_square(u, 0)
                    gate_and_add(1, u, "fc2_1", t, xo, vec2[:, :, 0, :], mlp_gated, x1, xo, x2_ready)
                    shift_rows(u, 0)
                if attn:
                    pool.wait_ge(gate1_in, (t + 1) * 32)
                    pool.wait_ge(x_res_ready, t + 1)
                    gate_and_add(0, t, "proj0", t, o, gate1, attn_gated, x_res, x1, x1_ready)
                    gate_and_add(1, t, "proj1", t, o, gate1, attn_gated, x_res, x1, x1_ready)
                    pool.wait_ge(ln2_step, (t + 1) * 3)
                    power(ve2[:], rs2[:], ln2_rstd)

            turns(pool, body)


STACK_LOADS = 32
PREP_WABS, PREP_SILU, PREP_CQ, PREP_CQT, PREP_TOK, PREP_ALL = 3, 6, 13, 19, 27, 28
ZEROS_ALL = 7
COND_ALL, CONSTS_ALL = 16 * 9, 16 * 8
MOD_COLS = [g * D + k * P for g in (0, 1, 3, 4) for k in range(KC)]


def kernel(x, cond_1024, L0_cond_W_qkv, L0_cond_b_qkv, L0_cond_W_proj, L0_cond_b_proj, L0_cond_W_fc1, L0_cond_b_fc1,
           L0_cond_W_fc2, L0_cond_b_fc2, L0_cond_W_ada, L0_cond_b_ada, L1_cond_w_proj, L1_cond_b_proj,
           L1_cond_rms_weight):
    import numpy as np
    import concourse.bacc as bacc
    from concourse.bass_utils import run_bass_kernel_spmd

    def chunks(w):
        w = np.asarray(w)
        return w.reshape(-1, P, w.shape[1]).transpose(1, 0, 2)

    def columns(b):
        return np.asarray(b).reshape(-1, P).T

    def line(b):
        return np.asarray(b).reshape(1, -1)

    ada_cols = columns(L0_cond_b_ada)
    mod_cols = [m // P for m in MOD_COLS]
    select = np.zeros((P, NI, P), np.float32)
    for a in range(2):
        for i in range(NI):
            for j in range(2):
                select[(a * NI + i) * 2 + j, i, j * SEQ:(j + 1) * SEQ] = 1.0
    arrays = {
        "x": np.asarray(x).reshape(BATCH * SEQ, D),
        "cT": chunks(np.asarray(cond_1024).T),
        "c": cond_1024,
        "w_qkv": chunks(L0_cond_W_qkv),
        "bT_qkv": columns(L0_cond_b_qkv)[:, 0:4],
        "b_v": line(L0_cond_b_qkv)[:, 2 * D:],
        "w_proj": chunks(L0_cond_W_proj),
        "b_proj": line(L0_cond_b_proj),
        "w_fc1": chunks(L0_cond_W_fc1),
        "bT_fc1": columns(L0_cond_b_fc1),
        "w_fc2": chunks(L0_cond_W_fc2),
        "b_fc2": line(L0_cond_b_fc2),
        "w_ada": chunks(L0_cond_W_ada),
        "bT_ada": ada_cols[:, mod_cols],
        "b_ada": line(L0_cond_b_ada),
        "w1T": chunks(np.asarray(L1_cond_w_proj).T),
        "b1": line(L1_cond_b_proj),
        "rms_w": line(L1_cond_rms_weight),
        "ident": np.eye(P, dtype=np.float32),
        "fold": np.tile(np.eye(SEQ, dtype=np.float32), (2, 1)),
        "select": select,
    }
    arrays = {k: np.ascontiguousarray(a) for k, a in arrays.items()}
    nc = bacc.Bacc("TRN2", target_bir_lowering=False, num_devices=1)
    args = {k: nc.dram_tensor(f"in_{k}", a.shape, mybir.dt.from_np(a.dtype), kind="ExternalInput").ap()
            for k, a in arrays.items()}
    result = nc.dram_tensor("out_rows", (BATCH * SEQ, D), F32, kind="ExternalOutput").ap()
    build(nc, out=result, **args)
    r = run_bass_kernel_spmd(nc, [{f"in_{k}": a for k, a in arrays.items()}], core_ids=[0])
    return r.results[0]["out_rows"].reshape(BATCH, SEQ, D)
```

```python
from contextlib import ExitStack

import concourse.bass as bass
from concourse import mybir

F32 = mybir.dt.float32
F32R = mybir.dt.float32r
BF16 = mybir.dt.bfloat16
ALU = mybir.AluOpType
ACT = mybir.ActivationFunctionType
AX = mybir.AxisListType

P = 128
BATCH, SEQ, D = 64, 64, 256
HEADS = 16
HD = D // HEADS
HID = 1024
TOK = 512
NB = TOK // SEQ
TILES = BATCH * SEQ // TOK
NS = TOK // P
KC = D // P
FC = HID // P
PAIRS = HEADS // 2
NI = PAIRS // KC
VW = HD + 1
NPR = 6
Q_RUNS, K_RUNS = ((0, 3, 0, 0), (3, 2, 1, 0), (5, 1, 2, 0)), ((0, 3, 0, 1), (3, 2, 0, 1), (5, 1, 0, 0))
ST = HD * NPR
QK = ("q0", "k0", "q1", "k1")
WHOLE = 4
LN_EPS, RMS_EPS, Q_EPS = 1e-6, 1e-6, 1e-5
ROUND = 1.5 * 2.0**23
SCALE = float(HD) ** -0.5


class Ring:

    def __init__(self, banks, filled, emptied, order, absent):
        self.banks, self.sem_filled, self.sem_emptied = banks, filled, emptied
        self.order, self.absent = order, absent

    def names(self, turn):
        return [n for n in self.order if not n.startswith(self.absent.get(turn, ()))]

    def place(self, name, turn):
        n = len(self.banks)
        if isinstance(turn, int):
            k = sum(len(self.names(before)) for before in range(-1, turn)) + self.names(turn).index(name)
            return k % n, k // n
        k = sum(len(self.names(before)) for before in (-1, 0, 1)) - 2 * len(self.order) + self.order.index(name)
        return k % n, turn * (len(self.order) // n) + k // n

    def bank(self, name, turn):
        return self.banks[self.place(name, turn)[0]]

    def free(self, name, turn):
        b, before = self.place(name, turn)
        return self.sem_emptied[b], before

    def filled(self, name, turn):
        b, before = self.place(name, turn)
        return self.sem_filled[b], before + 1

    def emptied(self, name, turn):
        b, before = self.place(name, turn)
        return self.sem_emptied[b], before + 1

    def signal_filled(self, name, turn):
        return self.sem_filled[self.place(name, turn)[0]], 1

    def signal_emptied(self, name, turn):
        return self.sem_emptied[self.place(name, turn)[0]], 1


def wait(eng, sem, value):
    if isinstance(value, int) and value <= 0:
        return
    eng.wait_ge(sem, value)


def row(ap, t):
    if isinstance(t, int):
        return ap[t]
    return ap[bass.ds(t, 1)].squeeze(0)


def build(nc, x, cT, c, w_qkv, bT_qkv, b_v, w_proj, b_proj, w_fc1, bT_fc1, w_fc2, b_fc2, w_ada, bT_ada,
          b_ada, w1T, b1, rms_w, ident, fold, select, out):
    with ExitStack() as ctx:
        def sb(name, shape, dt=F32):
            return ctx.enter_context(nc.sbuf_tensor(name, shape, dt))

        def sem(name):
            return ctx.enter_context(nc.semaphore(name))

        Wqkv = [sb(f"Wqkv_{n}", [P, KC, 3 * D], F32R) for n in ("hi", "lo")]
        Wp = sb("Wp", [P, KC, D])
        W1 = [sb(f"W1_{n}", [P, KC, HID], F32R) for n in ("hi", "lo")]
        W2 = [sb(f"W2_{n}", [P, FC, D], F32R) for n in ("hi", "lo")]
        bqk = sb("bqk", [P, 4])
        bqk_s = sb("bqk_s", [P, 4])
        b1T = sb("b1T", [P, FC])
        bv = sb("bv", [P, D])
        bp = sb("bp", [P, D])
        b2 = sb("b2", [P, D])
        idn = sb("idn", [P, P])
        fld = sb("fld", [P, SEQ])
        sel = sb("sel", [P, NI, P], F32R)
        halves = sb("halves", [P, NS])
        epss = sb("epss", [P, NS])
        one = sb("one", [P, 1])
        warm = sb("warm", [P, 1])
        waited = sb("waited", [P, 1])
        badaT = sb("badaT", [P, 8])
        cst = sb("cst", [BATCH, 4])
        wst = sb("wst", [P, 4])
        x_in = sb("x_in", [P, NS, D])
        x_res = sb("x_res", [P, NS, D])
        mod1 = sb("mod1", [P, 4, NB])
        gate1 = sb("gate1", [P, NS, D])
        st1 = sb("st1", [P, NS, 6])
        mv1 = sb("mv1", [P, NS, 2])
        ve1 = sb("ve1", [P, NS])
        rs1 = sb("rs1", [P, NS])
        hn = sb("hn", [P, NS, D])
        hS = sb("hS", [P, KC, TOK])
        hT1 = [sb(f"hT1_{n}", [P, KC, TOK], F32R) for n in ("hi", "lo")]
        whole = sb("whole", [P, WHOLE, TOK])
        qst = sb("qst", [P, HEADS, TOK], BF16)
        kst = sb("kst", [P, HEADS, TOK], BF16)
        v2 = sb("v2", [P, NB, PAIRS, 2, VW])
        nmax = sb("nmax", [P, KC, NI, NB])
        nmaxU = sb("nmaxU", [P, KC, NB, 2, NI, 2])
        pT = sb("pT", [P, PAIRS, TOK])
        rden = sb("rden", [P, NS, HEADS])
        parts = pT[:, 0:6, :].bitcast(BF16).rearrange("p a (x n) -> p (a x) n", x=2)
        qparts = parts[:, 0:6, :].rearrange("p (c a) n -> p c a n", c=KC)
        kparts = parts[:, 6:12, :].rearrange("p (c a) n -> p c a n", c=KC)
        mlp_rows = pT[:, 6:8, :].rearrange("p a (s f) -> p (a s) f", f=D)
        oT = hS
        o = hn
        hw1 = whole[:, 0:KC, :]
        hw2 = hn[:].rearrange("p s f -> p (s f)").rearrange("p (k n) -> p k n", k=KC)
        x1 = sb("x1", [P, NS, D])
        mod2 = sb("mod2", [P, 4, NB])
        vec2 = sb("vec2", [P, NS, 3, D])
        st2 = sb("st2", [P, NS, 6])
        mv2 = sb("mv2", [P, NS, 2])
        ve2 = sb("ve2", [P, NS])
        rs2 = sb("rs2", [P, NS])
        nm2 = sb("nm2", [P, NS])
        hT2 = [sb(f"hT2_{n}", [P, KC, TOK], F32R) for n in ("hi", "lo")]
        gT = [sb(f"gT_{n}", [P, FC, TOK], F32R) for n in ("hi", "lo")]
        nmaxT = gT[1][0:4 * NI, FC - KC:FC, :]
        xo = sb("xo", [P, NS, D])
        ssq = sb("ssq", [P, NS])
        msq = sb("msq", [P, NS])
        rms = sb("rms", [P, NS])
        Wada = qst[:, 0:12, :].bitcast(F32).rearrange("p a b -> p (a b)").rearrange("p (k n) -> p k n", k=KC)
        Wc, Wcq = pT[:, 0:KC, :], pT[:, KC:2 * KC, :]
        sel32 = pT[:, 4, :].rearrange("p (i q) -> p i q", i=NI)
        emb, bc, rmsw = pT[0:BATCH, 5, :], pT[0:BATCH, 6, :], pT[0:BATCH, 7, 0:D]
        tok_vec = o[0:BATCH, :, :]
        cTs, sil, sg, cqT = (whole[:, 0, k * P:(k + 1) * P].rearrange("p (k b) -> p k b", k=KC) for k in range(4))
        ones = whole[:, 1, 0:P]
        mod_all = whole[:, 2, :].rearrange("p (t v b) -> p t v b", t=TILES, v=8)
        bada, cb, cq = x1[0:BATCH, 0:2, :], x1[0:BATCH, 2, :], x1[0:BATCH, 3, :]
        Wqkv32 = kst[:, 0:6, :].bitcast(F32).rearrange("p a b -> p (a b)").rearrange("p (k n) -> p k n", k=KC)
        flat = vec2[:].rearrange("p s v f -> p (s v f)")
        W1_32 = flat[:, 0:KC * HID].rearrange("p (k n) -> p k n", k=KC)
        W2_32 = [flat[:, KC * HID:].rearrange("p (k n) -> p k n", n=D), xo]
        scr = nc.dram_tensor("scr", (BATCH, 4, D), F32, kind="Internal").ap()
        scr_mod = nc.dram_tensor("scr_mod", (P, TILES, 8, NB), F32, kind="Internal").ap()
        scr_qk = [[nc.dram_tensor(f"scr_{n}{c}", (3, HD, HEADS // KC, TOK), BF16, kind="Internal").ap() for n in "qk"]
                  for c in range(KC)]
        lg = ctx.enter_context(nc.psum_tensor("lg", [P, NI, TOK], F32))
        gb = [ctx.enter_context(nc.psum_tensor(f"gb{i}", [P, TOK], F32)) for i in range(2)]
        tb = [ctx.enter_context(nc.psum_tensor(f"tb{i}", [P, TOK], F32)) for i in range(2)]

        fc1_names = [f"fc1_{j}" for j in range(FC)]
        gemm = Ring(gb, [sem(f"gemm_filled{i}") for i in range(2)], [sem(f"gemm_emptied{i}") for i in range(2)],
                    ["q0", "k0", "q1", "k1", "v0", "v1", *fc1_names, "oT0", "oT1", "proj0", "proj1"],
                    {-1: ("",), 0: ("fc",), TILES: ("q", "k", "v", "oT", "proj")})
        misc = Ring(tb, [sem(f"misc_filled{i}") for i in range(2)], [sem(f"misc_emptied{i}") for i in range(2)],
                    ["fc2_1", "max0", "max1", "h1_0", "h1_1", "fc2_0"],
                    {-1: ("fc", "max"), 0: ("fc",), 1: ("fc2_1",), TILES - 1: ("h1",), TILES: ("max", "h1")})
        logit = Ring([lg], [sem("logits_filled")], [sem("logits_emptied")], ["s0", "s1", "sT0", "sT1", "pv"],
                     {-1: ("",), TILES: ("s", "pv")})

        consts_in = sem("consts_in")
        cond_in = sem("cond_in")
        weights_in = sem("weights_in")
        mlp_weights_in = sem("mlp_weights_in")
        prep = sem("prep")
        prep_act = sem("prep_act")
        prep_pe = sem("prep_pe")
        zeros_set = sem("zeros_set")
        scratch_out = sem("scratch_out")
        x_in_ready = sem("x_in_ready")
        mod1_in = sem("mod1_in")
        gate1_in = sem("gate1_in")
        mod2_in = sem("mod2_in")
        vec2_in = sem("vec2_in")
        x_res_ready = sem("x_res_ready")
        ln1_step = sem("ln1_step")
        ln1_rstd = sem("ln1_rstd")
        hn1_ready = sem("hn1_ready")
        hw1_ready = sem("hw1_ready")
        hT1_hi = sem("hT1_hi")
        hT1_ready = sem("hT1_ready")
        parts_step = sem("parts_step")
        parts_ready = sem("parts_ready")
        parts_out = [sem(f"parts_out_{n}{c}") for c in range(KC) for n in "qk"]
        stacks_in = [sem(f"stacks_in{c}") for c in range(KC)]
        nmax_step = sem("nmax_step")
        nmaxU_ready = sem("nmaxU_ready")
        rden_ready = sem("rden_ready")
        attn_gated = sem("attn_gated")
        x1_ready = sem("x1_ready")
        ln2_step = sem("ln2_step")
        ln2_rstd = sem("ln2_rstd")
        ln2_shift = sem("ln2_shift")
        hn2_ready = sem("hn2_ready")
        h2_filled = sem("h2_filled")
        h2_scaled = sem("h2_scaled")
        hw2_ready = sem("hw2_ready")
        hT2_hi = sem("hT2_hi")
        hT2_ready = sem("hT2_ready")
        g_hi = sem("g_hi")
        g_ready = sem("g_ready")
        w_hi = sem("w_hi")
        w_ready = sem("w_ready")
        x1_kept = sem("x1_kept")
        mlp_gated = sem("mlp_gated")
        high_ready = sem("high_ready")
        mid_ready = sem("mid_ready")
        x2_ready = sem("x2_ready")
        ssq_ready = sem("ssq_ready")
        msq_ready = sem("msq_ready")
        rms_ready = sem("rms_ready")
        ys_ready = sem("ys_ready")
        y_ready = sem("y_ready")
        y_stored = [sem(f"y_stored{k}") for k in range(2)]

        block = ctx.enter_context(nc.Block())

        def turns(eng, body):
            body(0, attn=True, mlp=False, late=False, more=True)
            body(1, attn=True, mlp=True, late=False, more=True)
            with eng.Fori(2, TILES - 1) as t:
                body(t, attn=True, mlp=True, late=True, more=True)
            body(TILES - 1, attn=True, mlp=True, late=True, more=False)
            body(TILES, attn=False, mlp=True, late=True, more=False)
            body(TILES + 1, attn=False, mlp=False, late=True, more=False)

        mlp_splits = [(W1_32[:, k, :], (W1[0][:, k, :], W1[1][:, k, :])) for k in range(KC)] + [
            (W2_32[k][:], (W2[0][:, k * FC // 2:(k + 1) * FC // 2, :], W2[1][:, k * FC // 2:(k + 1) * FC // 2, :]))
            for k in range(2)]

        x_v = x.rearrange("(t s p) f -> t p s f", s=NS, p=P)
        out_v = out.rearrange("(t s p) f -> t p s f", s=NS, p=P)
        scr_v = scr.rearrange("(t s h) v f -> t h s v f", s=NS, h=2)

        def mods(t, v):
            if isinstance(t, int):
                return scr_mod[:, t, v:v + 4, :]
            return scr_mod[:, bass.ds(t, 1), v:v + 4, :].squeeze(1)

        @block.sync
        def _(sp):
            for dst, src in ((cTs, cT), (cb, c), (Wada, w_ada), (Wc, w1T), (badaT, bT_ada)):
                sp.dma_start(dst[:], src).then_inc(cond_in, 16)
            for k, g in enumerate((2, 5)):
                sp.dma_start(bada[:, k, :], b_ada[:, g * D:(g + 1) * D].partition_broadcast(BATCH).rearrange(
                    "p a f -> p (a f)")).then_inc(cond_in, 16)
            sp.dma_start(bc[:], b1.partition_broadcast(BATCH).rearrange("p a f -> p (a f)")).then_inc(cond_in, 16)
            sp.dma_start(rmsw[:], rms_w.partition_broadcast(BATCH).rearrange("p a f -> p (a f)")).then_inc(cond_in, 16)
            sp.dma_start(x_in[:], x_v[0]).then_inc(x_in_ready, 16)
            for dst, src in ((idn, ident), (fld, fold), (sel32, select), (bqk, bT_qkv), (b1T, bT_fc1)):
                sp.dma_start(dst[:], src).then_inc(consts_in, 16)
            for dst, src in ((bv, b_v), (bp, b_proj), (b2, b_fc2)):
                sp.dma_start(dst[:], src.partition_broadcast(P).rearrange("p a f -> p (a f)")).then_inc(consts_in, 16)
            sp.dma_start(Wqkv32[:], w_qkv).then_inc(weights_in, 16)
            sp.dma_start(Wp[:], w_proj).then_inc(weights_in, 16)
            sp.dma_start(W1_32[:], w_fc1).then_inc(mlp_weights_in, 16)
            for k, half in enumerate(W2_32):
                sp.dma_start(half[:], w_fc2[:, k * FC // 2:(k + 1) * FC // 2, :]).then_inc(mlp_weights_in, 16)
            sp.wait_ge(prep, PREP_TOK)
            sp.dma_start(scr, tok_vec[:]).then_inc(scratch_out, 16)
            sp.dma_start(scr_mod, mod_all).then_inc(scratch_out, 16)
            sp.wait_ge(scratch_out, 32)
            sp.dma_start(mod1[:], mods(0, 0)).then_inc(mod1_in, 16)
            for h in range(2):
                sp.dma_start(gate1[h * SEQ:(h + 1) * SEQ, :, :], scr_v[0, h, :, 0, :].partition_broadcast(SEQ)
                             ).then_inc(gate1_in, 16)

            def store(tile, k):
                sp.wait_ge(y_ready, tile * 2 + k + 1)
                sp.dma_start(row(out_v, tile)[:, 2 * k:2 * k + 2, :], xo[:, 2 * k:2 * k + 2, :]
                             ).then_inc(y_stored[k], 16)

            def stacks(t, c):
                for n, parts in enumerate((qparts, kparts)):
                    k = 2 * c + n
                    for a in range(3):
                        if a == 0:
                            sp.wait_ge(high_ready, t * 4 + k + 1)
                        elif a == 1:
                            sp.wait_ge(mid_ready, t * 4 + k + 1)
                        else:
                            sp.wait_ge(parts_ready, t * 4 + k + 1)
                        sp.dma_start(scr_qk[c][n][a].rearrange("d h n -> h d n"), parts[:, c, a, :]
                                     ).then_inc(parts_out[k], 16)
                for n, (stack, runs) in enumerate(((qst, Q_RUNS), (kst, K_RUNS))):
                    sp.wait_ge(parts_out[2 * c + n], (t + 1) * 48)
                    for first, blocks, part, step in runs:
                        if step:
                            src = scr_qk[c][n][part:part + blocks].rearrange("a d h n -> (a d) (h n)")
                        else:
                            src = scr_qk[c][n][part:part + 1].rearrange("a d h n -> a d (h n)").broadcast_to(
                                [blocks, HD, TOK * HEADS // KC])
                        sp.dma_start(stack[first * HD:(first + blocks) * HD, c * HEADS // KC:(c + 1) * HEADS // KC, :],
                                     src).then_inc(stacks_in[c], 16)

            def body(t, attn, mlp, late, more):
                u, w = t - 1, t - 2
                if mlp:
                    wait(sp, hT2_ready, u * KC)
                    sp.dma_start(mod2[:], mods(u, 4)).then_inc(mod2_in, 16)
                if attn:
                    if not (isinstance(t, int) and t == 0):
                        sp.wait_ge(*logit.filled("sT1", u))
                    stacks(t, 0)
                if attn:
                    stacks(t, 1)
                if late:
                    store(w, 0)
                if mlp and attn:
                    sp.wait_ge(attn_gated, t * 2)
                    for h in range(2):
                        sp.dma_start(gate1[h * SEQ:(h + 1) * SEQ, :, :],
                                     row(scr_v, t)[h, :, 0, :].partition_broadcast(SEQ)).then_inc(gate1_in, 16)
                if more:
                    sp.wait_ge(hn1_ready, (t + 1) * NS)
                    sp.wait_ge(x_res_ready, t + 1)
                    sp.dma_start(x_in[:], row(x_v, t + 1)).then_inc(x_in_ready, 16)
                    sp.wait_ge(hT1_ready, (t + 1) * KC)
                    sp.dma_start(mod1[:], mods(t + 1, 0)).then_inc(mod1_in, 16)
                if late:
                    store(w, 1)
                if mlp:
                    if isinstance(u, int) and u == 0:
                        sp.wait_ge(w_ready, W_SPLITS)
                    for h in range(2):
                        sp.dma_start(vec2[h * SEQ:(h + 1) * SEQ, :, :, :],
                                     row(scr_v, u)[h, :, 1:4, :].partition_broadcast(SEQ)).then_inc(vec2_in, 16)

            turns(sp, body)
            sp.wait_ge(y_stored[0], 16 * TILES)
            sp.wait_ge(y_stored[1], 16 * TILES)

        @block.tensor
        def _(pe):
            mm = nc.tensor.matmul
            pe.wait_ge(prep, PREP_WABS)
            mm(tb[1][:, 0:2], ones[:], wst[:, 0:2], start=True, stop=True).then_inc(prep_pe, 1)
            pe.wait_ge(prep, PREP_SILU)
            pe.wait_ge(cond_in, COND_ALL)
            for n, col in enumerate(MOD_COLS):
                for k in range(KC):
                    last = mm(gb[0][:, n * BATCH:(n + 1) * BATCH], Wada[:, k, col:col + P], sil[:, k, :],
                              start=(k == 0), stop=(k == KC - 1))
            last.then_inc(prep_pe, 1)
            for n, g in enumerate((2, 5)):
                for k in range(KC):
                    last = mm(gb[1][0:BATCH, n * D:(n + 1) * D], sil[:, k, :], Wada[:, k, g * D:(g + 1) * D],
                              start=(k == 0), stop=(k == KC - 1))
            last.then_inc(prep_pe, 1)
            pe.wait_ge(prep, PREP_CQ)
            pe.wait_ge(consts_in, CONSTS_ALL)
            for k in range(KC):
                last = nc.tensor.transpose(tb[0][:, k * BATCH:(k + 1) * BATCH], cq[:, k * P:(k + 1) * P],
                                           idn[0:BATCH, 0:BATCH])
            last.then_inc(prep_pe, 1)
            pe.wait_ge(prep, PREP_CQT)
            for k in range(KC):
                last = mm(lg[0:BATCH, 0, :], cqT[:, k, :], Wcq[:, k, :], start=(k == 0), stop=(k == KC - 1))
            last.then_inc(prep_pe, 1)
            pe.wait_ge(prep, PREP_ALL)
            pe.wait_ge(zeros_set, ZEROS_ALL)

            def transpose(dst, src, c):
                for s in range(NS):
                    last = nc.tensor.transpose(dst[:, s * P:(s + 1) * P], src[:, s, c * P:(c + 1) * P], idn[:])
                return last

            def to_features(ring, name, t, src):
                wait(pe, *ring.free(name, t))
                transpose(ring.bank(name, t), src, int(name[-1])).then_inc(*ring.signal_filled(name, t))

            def product(dst, stationary, moving, chunks):
                pairs = ((0, 0), (0, 1), (1, 0))
                for k in range(chunks):
                    for n, (a, b) in enumerate(pairs):
                        last = mm(dst, stationary(a, k), moving(b, k), start=(k == 0 and n == 0),
                                  stop=(k == chunks - 1 and n == len(pairs) - 1))
                return last

            def columns_out(name, t, w, col, src):
                wait(pe, *gemm.free(name, t))
                product(gemm.bank(name, t)[:], lambda a, k: w[a][:, k, col:col + P], lambda b, k: src[b][:, k, :], KC
                        ).then_inc(*gemm.signal_filled(name, t))

            def fc1(names, t):
                for n in names:
                    columns_out(n, t, W1, int(n[4:]) * P, hT2)

            def rows_out(ring, name, t, src, w, col, chunks):
                for s in range(2):
                    block_out(ring, name, t, s, src, w, col, chunks)

            def block_out(ring, name, t, s, src, w, col, chunks):
                if s == 0:
                    wait(pe, *ring.free(name, t))
                tok = (2 * int(name[-1]) + s) * P
                last = product(ring.bank(name, t)[:, s * D:(s + 1) * D], lambda a, k: src[a][:, k, tok:tok + P],
                               lambda b, k: w[b][:, k, col:col + D], chunks)
                if s == 1:
                    last.then_inc(*ring.signal_filled(name, t))

            def project(name, t):
                h = int(name[-1])
                wait(pe, *gemm.free(name, t))
                for s in range(2):
                    tok = (2 * h + s) * P
                    for k in range(KC):
                        last = mm(gemm.bank(name, t)[:, s * D:(s + 1) * D], oT[:, k, tok:tok + P], Wp[:, k, :],
                                  start=(k == 0), stop=(k == KC - 1))
                last.then_inc(*gemm.signal_filled(name, t))

            def logits(name, t):
                c = int(name[-1])
                st = name.startswith("sT")
                wait(pe, *logit.free(name, t))
                if st:
                    pe.wait_ge(*misc.emptied(f"max{c}", t))
                    for i in range(NI):
                        mm(lg[:, i, :], sel[0:4 * NI, i, :], nmaxT[:, c, :], start=True, stop=False, skip_group_check=True)
                stat, mov = (kst, qst) if st else (qst, kst)
                for j in range(2):
                    for b in range(NB):
                        tk = slice(b * SEQ, (b + 1) * SEQ)
                        for i in range(NI):
                            head = 2 * (c * NI + i) + j
                            last = mm(lg[j * SEQ:(j + 1) * SEQ, i, tk], stat[0:ST, head, tk], mov[0:ST, head, tk],
                                      start=(not st), stop=True, skip_group_check=True)
                last.then_inc(*logit.signal_filled(name, t))

            def turn_max(c, t):
                n = f"max{c}"
                pe.wait_ge(nmaxU_ready, t * KC + c + 1)
                wait(pe, *misc.free(n, t))
                for b in range(NB):
                    last = mm(misc.bank(n, t)[0:4 * NI, b * SEQ:(b + 1) * SEQ],
                              nmaxU[:, c, b, :, :, :].rearrange("p a i j -> p (a i j)"), fld[:],
                              start=True, stop=True)
                last.then_inc(*misc.signal_filled(n, t))

            def rows_of_next(turn):
                pe.wait_ge(hn1_ready, (turn + 2) * NS)
                to_features(misc, "h1_0", turn, hn)
                to_features(misc, "h1_1", turn, hn)

            rows_of_next(-1)

            def body(t, attn, mlp, late, more):
                u = t - 1
                if attn:
                    pe.wait_ge(hT1_ready, (t + 1) * KC)
                    for n in QK:
                        columns_out(n, t, Wqkv, (D if n[0] == "k" else 0) + int(n[1]) * P, hT1)
                    rows_out(gemm, "v0", t, hT1, Wqkv, 2 * D, KC)
                    rows_out(gemm, "v1", t, hT1, Wqkv, 2 * D, KC)
                if late:
                    block_out(misc, "fc2_1", t, 0, gT, W2, 0, FC)
                if mlp:
                    pe.wait_ge(hn2_ready, (u + 1) * NS)
                    for c in range(KC):
                        last = transpose(lg[:, c, :], hn, c)
                    last.then_inc(h2_filled, 1)
                if late:
                    block_out(misc, "fc2_1", t, 1, gT, W2, 0, FC)
                if attn:
                    if mlp:
                        pe.wait_ge(h2_scaled, (u + 1) * KC)
                    pe.wait_ge(stacks_in[0], (t + 1) * STACK_LOADS)
                    logits("s0", t)
                if mlp:
                    pe.wait_ge(w_ready, W_SPLITS)
                    pe.wait_ge(hT2_ready, (u + 1) * KC)
                    fc1(fc1_names[0:3], t)
                if attn:
                    pe.wait_ge(stacks_in[1], (t + 1) * STACK_LOADS)
                    logits("s1", t)
                    turn_max(0, t)
                if mlp:
                    fc1(fc1_names[3:6], t)
                if attn:
                    logits("sT0", t)
                    turn_max(1, t)
                if mlp:
                    fc1(fc1_names[6:7], t)
                if attn:
                    logits("sT1", t)
                if more:
                    rows_of_next(t)
                if mlp:
                    fc1(fc1_names[7:8], t)
                if attn:
                    pe.wait_ge(*gemm.emptied("v0", t))
                    pe.wait_ge(*gemm.emptied("v1", t))
                    wait(pe, *logit.free("pv", t))
                    for b in range(NB):
                        half = slice(b % 2 * SEQ, (b % 2 + 1) * SEQ)
                        for p in range(PAIRS):
                            last = mm(lg[half, b // 2, p * 2 * VW:(p + 1) * 2 * VW], pT[:, p, b * SEQ:(b + 1) * SEQ],
                                      v2[:, b, p, :, :].rearrange("p j e -> p (j e)"), start=True, stop=True)
                    last.then_inc(*logit.signal_filled("pv", t))
                if mlp:
                    pe.wait_ge(g_ready, (u + 1) * FC)
                    block_out(misc, "fc2_0", t, 0, gT, W2, 0, FC)
                if attn:
                    pe.wait_ge(*logit.emptied("pv", t))
                    to_features(gemm, "oT0", t, o)
                    to_features(gemm, "oT1", t, o)
                if mlp:
                    block_out(misc, "fc2_0", t, 1, gT, W2, 0, FC)
                if attn:
                    pe.wait_ge(weights_in, 32)
                    pe.wait_ge(*gemm.emptied("oT0", t))
                    pe.wait_ge(*gemm.emptied("oT1", t))
                    project("proj0", t)
                    project("proj1", t)

            turns(pe, body)

        @block.scalar
        def _(act):
            act.wait_ge(cond_in, COND_ALL)
            nc.scalar.activation(sg[:], cTs[:], ACT.Exp, scale=-1.0).then_inc(prep_act, 1)
            act.wait_ge(consts_in, CONSTS_ALL)
            nc.scalar.mul(bqk_s[:], bqk[:], SCALE).then_inc(prep_act, 1)
            act.wait_ge(prep_act, 2)

            def squares(tile, k):
                act.wait_ge(x2_ready, tile * 2 + k + 1)
                for s in (2 * k, 2 * k + 1):
                    nc.scalar.activation(mlp_rows[:, s, :], xo[:, s, :], ACT.Square, scale=float(D) ** -0.5,
                                         accum_out=ssq[:, s:s + 1]).then_inc(ssq_ready, 1)

            def normalised(t):
                act.wait_ge(ln2_shift, t + 1)
                for s in (0, 1):
                    nc.scalar.activation(hn[:, s, :], x1[:, s, :], ACT.Identity, bias=nm2[:, s:s + 1],
                                         scale=rs2[:, s:s + 1]).then_inc(hn2_ready, 1)

            def body(t, attn, mlp, late, more):
                u, w = t - 1, t - 2

                def queries_keys(n):
                    c = int(n[1])
                    act.wait_ge(*gemm.filled(n, t))
                    k = QK.index(n)
                    if n[0] == "q":
                        ins = nc.scalar.activation(whole[:, k, :], gemm.bank(n, t)[:], ACT.Identity,
                                                   bias=bqk_s[:, c:c + 1], scale=SCALE)
                    else:
                        ins = nc.scalar.activation(whole[:, k, :], gemm.bank(n, t)[:], ACT.Identity,
                                                   bias=bqk[:, KC + c:KC + c + 1])
                    ins.then_inc(*gemm.signal_emptied(n, t))
                    act.wait_ge(*gemm.emptied(n, t))
                    nc.scalar.copy((kparts if n[0] == "k" else qparts)[:, c, 0, :], whole[:, k, :]
                                   ).then_inc(high_ready, 1)

                def max_rows():
                    act.wait_ge(*misc.filled("max0", t))
                    nc.scalar.copy(nmaxT[:, 0, :], misc.bank("max0", t)[0:4 * NI, :]
                                   ).then_inc(*misc.signal_emptied("max0", t))

                def probabilities(c):
                    act.wait_ge(*logit.filled(f"sT{c}", t))
                    nc.scalar.activation(pT[:, c * NI:(c + 1) * NI, :], lg[:], ACT.Exp
                                         ).then_inc(*logit.signal_emptied(f"sT{c}", t))

                def gelu(names):
                    for n in names:
                        j = int(n[4:])
                        if j >= WHOLE:
                            act.wait_ge(g_ready, u * FC + j - WHOLE + 1)
                        elif attn:
                            act.wait_ge(parts_ready, t * 4 + j + 1)
                        act.wait_ge(*gemm.filled(n, t))
                        nc.scalar.activation(whole[:, j % WHOLE, :], gemm.bank(n, t)[:], ACT.Gelu_apprx_tanh,
                                             bias=b1T[:, j:j + 1]).then_inc(*gemm.signal_emptied(n, t))

                if attn:
                    queries_keys("q0")
                    queries_keys("k0")
                    queries_keys("q1")
                    queries_keys("k1")
                    wait(act, x1_ready, t * 2)
                    act.wait_ge(x_in_ready, (t + 1) * 16)
                    nc.scalar.copy(x_res[:], x_in[:]).then_inc(x_res_ready, 1)
                if mlp:
                    normalised(u)
                if late:
                    squares(w, 0)
                if mlp:
                    gelu(fc1_names[0:2])
                if late:
                    squares(w, 1)
                if mlp:
                    gelu(fc1_names[2:3])
                if attn:
                    max_rows()
                if mlp:
                    gelu(fc1_names[3:6])
                if attn:
                    nc.scalar.activation(warm[:], halves[:, 0:1], ACT.Exp)
                    probabilities(0)
                    probabilities(1)
                if mlp:
                    gelu(fc1_names[6:8])
                    for k in range(2):
                        wait(act, y_stored[k], u * 16)
                    nc.scalar.copy(xo[:], x1[:]).then_inc(x1_kept, 1)
                if attn:
                    if more:
                        act.wait_ge(hT1_ready, (t + 2) * KC)
                    for c in range(KC):
                        act.wait_ge(*gemm.filled(f"oT{c}", t))
                        nc.scalar.copy(oT[:, c, :], gemm.bank(f"oT{c}", t)[:]
                                       ).then_inc(*gemm.signal_emptied(f"oT{c}", t))

            turns(act, body)

        @block.vector
        def _(dve):
            v = nc.vector
            steps = [0]

            def link(ins):
                steps[0] += 1
                ins.then_inc(prep, 1)
                dve.wait_ge(prep, steps[0])

            v.memset(v2[:], 0.0).then_inc(zeros_set, 1)
            v.memset(nmaxU[:], 0.0).then_inc(zeros_set, 1)
            v.memset(halves[:], -0.5).then_inc(zeros_set, 1)
            v.memset(epss[:], RMS_EPS).then_inc(zeros_set, 1)
            v.memset(one[:], 1.0).then_inc(zeros_set, 1)
            dve.wait_ge(zeros_set, 5)
            v.memset(v2[0:SEQ, :, :, 0, HD:VW], 1.0).then_inc(zeros_set, 1)
            v.memset(v2[SEQ:P, :, :, 1, HD:VW], 1.0).then_inc(zeros_set, 1)
            link(v.memset(wst[:], 0.0))
            link(v.memset(ones[:], 1.0))
            dve.wait_ge(cond_in, COND_ALL)
            link(v.tensor_reduce(wst[:, 0:1], Wc[:].rearrange("p k n -> p (k n)"), AX.X, ALU.add,
                                 apply_absolute_value=True))
            assert steps[0] == PREP_WABS
            dve.wait_ge(prep_act, 1)
            link(v.tensor_scalar(sil[:], sg[:], 1.0, None, ALU.add))
            link(v.reciprocal(sg[:], sil[:]))
            link(v.tensor_tensor(sil[:], cTs[:], sg[:], ALU.mult))
            assert steps[0] == PREP_SILU
            link(v.tensor_reduce(cst[:, 0:1], cb[:], AX.X, ALU.max, apply_absolute_value=True))
            link(v.tensor_scalar(cst[:, 0:1], cst[:, 0:1], Q_EPS, None, ALU.max))
            link(v.reciprocal(cst[:, 1:2], cst[:, 0:1]))
            link(v.tensor_scalar(cst[:, 1:2], cst[:, 1:2], 127.0, None, ALU.mult))
            link(v.tensor_scalar(cq[:], cb[:], cst[:, 1:2], ROUND, ALU.mult, ALU.add))
            link(v.tensor_scalar(cq[:], cq[:], ROUND, 127.0, ALU.subtract, ALU.min))
            link(v.tensor_scalar(cq[:], cq[:], -128.0, None, ALU.max))
            assert steps[0] == PREP_CQ
            dve.wait_ge(prep_pe, 1)
            link(v.tensor_scalar(wst[:, 2:3], tb[1][:, 0:1], 1.0 / (2 * D * D), Q_EPS, ALU.mult, ALU.max))
            link(v.reciprocal(wst[:, 3:4], wst[:, 2:3]))
            link(v.tensor_scalar(Wcq[:], Wc[:], wst[:, 3:4], ROUND, ALU.mult, ALU.add))
            link(v.tensor_scalar(Wcq[:], Wcq[:], ROUND, 1.0, ALU.subtract, ALU.min))
            link(v.tensor_scalar(Wcq[:], Wcq[:], -1.0, None, ALU.max))
            dve.wait_ge(prep_pe, 4)
            link(v.tensor_copy(cqT[:].rearrange("p k b -> p (k b)"), tb[0][:, 0:KC * BATCH]))
            assert steps[0] == PREP_CQT
            link(v.tensor_tensor(mod_all[:].rearrange("p t v b -> p v t b"),
                                 gb[0][:].rearrange("p (v t b) -> p v t b", v=8, t=TILES),
                                 badaT[:].unsqueeze(2).unsqueeze(3).broadcast_to([P, 8, TILES, NB]), ALU.add))
            scales = mod_all[:].rearrange("p t (w z) b -> p w t (z b)", w=4)
            for w in (1, 3):
                link(v.tensor_scalar(scales[:, w, :, :], scales[:, w, :, :], 1.0, None, ALU.add))
            link(v.tensor_tensor(tok_vec[:, 0:2, :], gb[1][0:BATCH, :].rearrange("p (v f) -> p v f", v=2), bada[:],
                                 ALU.add))
            link(v.tensor_scalar(cst[:, 2:3], cst[:, 0:1], 1.0 / 127.0, wst[0:BATCH, 2:3], ALU.mult, ALU.mult))
            dve.wait_ge(prep_pe, 5)
            link(v.scalar_tensor_tensor(emb[:], lg[0:BATCH, 0, :], cst[:, 2:3], bc[:], ALU.mult, ALU.add))
            link(v.scalar_tensor_tensor(tok_vec[:, 2, :], emb[:, 0:D], 1.0, rmsw[:], ALU.add, ALU.mult))
            link(v.tensor_copy(tok_vec[:, 3, :], emb[:, D:2 * D]))
            assert steps[0] == PREP_TOK
            dve.wait_ge(consts_in, CONSTS_ALL)
            link(v.tensor_copy(sel[:], sel32[:]))
            assert steps[0] == PREP_ALL
            dve.wait_ge(weights_in, 32)
            for k in range(KC):
                v.tensor_copy(Wqkv[0][:, k, :], Wqkv32[:, k, :]).then_inc(w_hi, 1)
            for k in range(KC):
                dve.wait_ge(w_hi, k + 1)
                v.tensor_tensor(Wqkv[1][:, k, :], Wqkv32[:, k, :], Wqkv[0][:, k, :], ALU.subtract
                                ).then_inc(w_ready, 1)

            def statistics(t, src, st, mv, ve, nm, step):
                for s in range(NS):
                    last = v.bn_stats(st[:, s, :], src[:, s, :])
                last.then_inc(step, 1)
                dve.wait_ge(step, t * 3 + 1)
                v.memset(waited[:], 0.0)
                for s in range(NS):
                    last = v.bn_aggr(mv[:, s, :], st[:, s, :])
                last.then_inc(step, 1)
                dve.wait_ge(step, t * 3 + 2)
                if nm is not None:
                    v.tensor_scalar(nm[:], mv[:, :, 0], -1.0, None, ALU.mult)
                v.tensor_scalar(ve[:], mv[:, :, 1], LN_EPS, None, ALU.add).then_inc(step, 1)

            def columns(banks, mod, dst, his):
                for c, (bank, filled, emptied, _) in enumerate(banks):
                    dve.wait_ge(*filled)
                    v.tensor_tensor(hS[:, c, :].rearrange("p (b n) -> p b n", b=NB),
                                    bank.rearrange("p (b n) -> p b n", b=NB),
                                    mod[:, KC + c, :].unsqueeze(2).broadcast_to([P, NB, SEQ]), ALU.mult
                                    ).then_inc(*emptied)
                for c, (*_, scaled) in enumerate(banks):
                    dve.wait_ge(*scaled)
                    v.tensor_tensor(dst[0][:, c, :].rearrange("p (b n) -> p b n", b=NB),
                                    hS[:, c, :].rearrange("p (b n) -> p b n", b=NB),
                                    mod[:, c, :].unsqueeze(2).broadcast_to([P, NB, SEQ]), ALU.add).then_inc(his, 1)

            def columns_rest(tile, dst, his, hw, whole_ready, ready):
                dve.wait_ge(his, (tile + 1) * KC)
                for c in range(KC):
                    dve.wait_ge(whole_ready, tile * KC + c + 1)
                    v.tensor_tensor(dst[1][:, c, :], hw[:, c, :], dst[0][:, c, :], ALU.subtract).then_inc(ready, 1)

            def rows_in(ring, name, t, bias, dst):
                dve.wait_ge(*ring.filled(name, t))
                v.tensor_tensor(dst, ring.bank(name, t)[:].rearrange("p (s f) -> p s f", s=2),
                                bias[:].unsqueeze(1).broadcast_to([P, 2, D]), ALU.add
                                ).then_inc(*ring.signal_emptied(name, t))

            def ln1(t):
                dve.wait_ge(x_in_ready, (t + 1) * 16)
                statistics(t, x_in, st1, mv1, ve1, None, ln1_step)

            def normalised(t, blocks, src, mv, rs, rstd, ready):
                dve.wait_ge(rstd, t + 1)
                for s in blocks:
                    v.tensor_scalar(hn[:, s, :], src[:, s, :], mv[:, s, 0:1], rs[:, s:s + 1], ALU.subtract, ALU.mult
                                    ).then_inc(ready, 1)

            def ln1_rows(t):
                normalised(t, range(NS), x_in, mv1, rs1, ln1_rstd, hn1_ready)

            def columns_of_next(turn):
                dve.wait_ge(mod1_in, (turn + 2) * 16)
                columns([(misc.bank(n, turn)[:], misc.filled(n, turn), misc.signal_emptied(n, turn),
                          misc.emptied(n, turn)) for n in ("h1_0", "h1_1")], mod1, hT1, hT1_hi)

            def columns_of_next_rest(turn):
                columns_rest(turn + 1, hT1, hT1_hi, hw1, hw1_ready, hT1_ready)

            dve.wait_ge(scratch_out, 32)
            ln1(0)
            ln1_rows(0)
            columns_of_next(-1)
            columns_of_next_rest(-1)

            def body(t, attn, mlp, late, more):
                u, w = t - 1, t - 2

                def split(n):
                    c, k = int(n[1]), QK.index(n)
                    left, dst = whole[:, k, :], (kparts if n[0] == "k" else qparts)[:, c, :, :]
                    dve.wait_ge(high_ready, t * 4 + k + 1)
                    v.tensor_tensor(left, left, dst[:, 0, :], ALU.subtract).then_inc(parts_step, 1)
                    dve.wait_ge(parts_step, t * 4 + k + 1)
                    v.tensor_copy(dst[:, 1, :], left).then_inc(mid_ready, 1)
                    if c == 0:
                        dve.wait_ge(mid_ready, t * 4 + k + 1)
                        v.tensor_tensor(dst[:, 2, :], left, dst[:, 1, :], ALU.subtract).then_inc(parts_ready, 1)

                def attended():
                    heads = lg[:, :, 0:HEADS * VW].rearrange("p s (h e) -> p s h e", e=VW)
                    dve.wait_ge(*logit.filled("pv", t))
                    v.reciprocal(rden[:], heads[:, :, :, HD]).then_inc(rden_ready, 1)
                    wait(dve, x1_ready, t * 2)
                    dve.wait_ge(rden_ready, t + 1)
                    v.tensor_tensor(o[:].rearrange("p s (h d) -> p s h d", d=HD), heads[:, :, :, 0:HD],
                                    rden[:].unsqueeze(3).broadcast_to([P, NS, HEADS, HD]), ALU.mult
                                    ).then_inc(*logit.signal_emptied("pv", t))

                def rest(names):
                    for n in names:
                        j = int(n[4:])
                        dve.wait_ge(g_hi, u * FC + j + 1)
                        v.tensor_tensor(gT[1][:, j, :], whole[:, j % WHOLE, :], gT[0][:, j, :], ALU.subtract
                                        ).then_inc(g_ready, 1)

                def maxima(c):
                    dve.wait_ge(*logit.filled(f"s{c}", t))
                    v.tensor_reduce(nmax[:, c, :, :], lg[:].rearrange("p i (b m) -> p i b m", b=NB), AX.X, ALU.max,
                                    negate=True).then_inc(*logit.signal_emptied(f"s{c}", t))
                    dve.wait_ge(*logit.emptied(f"s{c}", t))
                    halves_of = ((0, slice(0, SEQ)), (1, slice(SEQ, P)))
                    for j, r in halves_of:
                        v.tensor_copy(nmaxU[r, c, :, 0, :, j].bitcast(F32R),
                                      nmax[r, c, :, :].rearrange("p i b -> p b i")).then_inc(nmax_step, 1)
                    dve.wait_ge(nmax_step, t * 4 + 2 * c + 2)
                    for j, r in halves_of:
                        last = v.tensor_tensor(nmaxU[r, c, :, 1, :, j], nmax[r, c, :, :].rearrange("p i b -> p b i"),
                                               nmaxU[r, c, :, 0, :, j], ALU.subtract)
                    last.then_inc(nmaxU_ready, 1)

                def mlp_weights():
                    for k, (src, w) in enumerate(mlp_splits):
                        dve.wait_ge(w_hi, KC + k + 1)
                        v.tensor_tensor(w[1], src, w[0], ALU.subtract).then_inc(w_ready, 1)

                def scale_rows(tile, k):
                    dve.wait_ge(rms_ready, tile * 2 + k + 1)
                    for s in (2 * k, 2 * k + 1):
                        last = v.scalar_tensor_tensor(xo[:, s, :], xo[:, s, :], rms[:, s:s + 1], vec2[:, s, 1, :],
                                                      ALU.mult, ALU.mult)
                    last.then_inc(ys_ready, 1)

                def values(n):
                    dve.wait_ge(*gemm.filled(n, t))
                    halves_of = ((0, slice(0, SEQ)), (1, slice(SEQ, P)))
                    for h, r in halves_of:
                        for j, to in halves_of:
                            last = v.tensor_tensor(
                                v2[to, :, :, j, 0:HD].rearrange("p (a h) q d -> p a h q d", h=2)[
                                    :, 2 * int(n[1]):2 * int(n[1]) + 2, h, :, :],
                                gemm.bank(n, t)[r, :].rearrange("p (a q j d) -> p a q j d", a=2, j=2, d=HD)[
                                    :, :, :, j, :],
                                bv[r, :].rearrange("p (q j d) -> p q j d", j=2, d=HD)[:, :, j, :].unsqueeze(1)
                                .broadcast_to([SEQ, 2, PAIRS, HD]), ALU.add)
                    last.then_inc(*gemm.signal_emptied(n, t))

                if attn:
                    split("q0")
                    split("k0")
                if mlp:
                    dve.wait_ge(x1_ready, (u + 1) * 2)
                    statistics(u, x1, st2, mv2, ve2, nm2, ln2_step)
                if attn:
                    split("q1")
                if mlp:
                    normalised(u, (2, 3), x1, mv2, rs2, ln2_rstd, hn2_ready)
                if attn:
                    split("k1")
                if mlp:
                    dve.wait_ge(mod2_in, (u + 1) * 16)
                    columns([(lg[:, c, :], (h2_filled, u + 1), (h2_scaled, 1), (h2_scaled, u * KC + c + 1))
                             for c in range(KC)], mod2, hT2, hT2_hi)
                if attn:
                    values("v0")
                if mlp:
                    columns_rest(u, hT2, hT2_hi, hw2, hw2_ready, hT2_ready)
                if attn:
                    values("v1")
                if late:
                    rows_in(misc, "fc2_1", t, b2, mlp_rows[:, 2:4, :])
                if attn:
                    maxima(0)
                if late:
                    scale_rows(w, 0)
                if mlp:
                    rest(fc1_names[0:2])
                if attn:
                    maxima(1)
                if late:
                    scale_rows(w, 1)
                if more:
                    ln1(t + 1)
                if mlp:
                    rest(fc1_names[2:4])
                if attn:
                    dve.wait_ge(*misc.filled("max1", t))
                    v.tensor_copy(nmaxT[:, 1, :], misc.bank("max1", t)[0:4 * NI, :]
                                  ).then_inc(*misc.signal_emptied("max1", t))
                if mlp:
                    rest(fc1_names[4:5])
                if more:
                    ln1_rows(t + 1)
                if mlp:
                    rest(fc1_names[5:6])
                elif attn:
                    mlp_weights()
                if more:
                    columns_of_next(t)
                if mlp:
                    rest(fc1_names[6:8])
                if attn:
                    attended()
                if more:
                    columns_of_next_rest(t)
                if mlp:
                    rows_in(misc, "fc2_0", t, b2, mlp_rows[:, 0:2, :])
                if attn:
                    dve.wait_ge(*gemm.filled("oT0", t))
                    dve.wait_ge(*gemm.filled("oT1", t))
                    dve.wait_ge(gate1_in, (t + 1) * 32)
                    for k, n in enumerate(("proj0", "proj1")):
                        rows = o[:, 2 * k:2 * k + 2, :]
                        rows_in(gemm, n, t, bp, rows)
                        dve.wait_ge(*gemm.emptied(n, t))
                        v.tensor_tensor(rows, rows, gate1[:, 2 * k:2 * k + 2, :], ALU.mult).then_inc(attn_gated, 1)

            turns(dve, body)

        @block.gpsimd
        def _(pool):
            g = nc.gpsimd

            def power(src, dst, ready):
                g.tensor_tensor(dst, src, halves[:, 0:src.shape[1]], ALU.pow).then_inc(ready, 1)

            def shift_columns(t, mod, mod_in, scaled, hw, ready):
                pool.wait_ge(mod_in, (t + 1) * 16)
                for c in range(KC):
                    pool.wait_ge(*scaled[c])
                    g.tensor_tensor(hw[:, c, :].rearrange("p (b n) -> p b n", b=NB),
                                    hS[:, c, :].rearrange("p (b n) -> p b n", b=NB),
                                    mod[:, c, :].unsqueeze(2).broadcast_to([P, NB, SEQ]), ALU.add).then_inc(ready, 1)

            def gate_and_add(k, t, there, acc, gate, gated, res, dst, ready):
                s = slice(2 * k, 2 * k + 2)
                rows = acc[:, s, :]
                pool.wait_ge(*there)
                g.tensor_tensor(rows, rows, gate[:, s, :], ALU.mult).then_inc(gated, 1)
                pool.wait_ge(gated, t * 2 + k + 1)
                g.tensor_tensor(dst[:, s, :], res[:, s, :], rows, ALU.add).then_inc(ready, 1)

            def scale_and_shift(t, step, ve, rs, nm, rstd, shift):
                pool.wait_ge(step, (t + 1) * 3)
                power(ve[:], rs[:], rstd)
                pool.wait_ge(rstd, t + 1)
                g.tensor_tensor(nm[:], nm[:], rs[:], ALU.mult).then_inc(shift, 1)

            def next_rstd(turn):
                pool.wait_ge(ln1_step, (turn + 2) * 3)
                power(ve1[:], rs1[:], ln1_rstd)

            def next_columns(turn):
                shift_columns(turn + 1, mod1, mod1_in, [misc.emptied(n, turn) for n in ("h1_0", "h1_1")], hw1,
                              hw1_ready)

            pool.wait_ge(zeros_set, ZEROS_ALL)
            next_rstd(-1)
            next_columns(-1)

            def body(t, attn, mlp, late, more):
                u, w = t - 1, t - 2

                def mean_square(tile, k):
                    s = slice(2 * k, 2 * k + 2)
                    pool.wait_ge(ssq_ready, tile * NS + 2 * k + 2)
                    g.tensor_tensor(msq[:, s], ssq[:, s], epss[:, s], ALU.add).then_inc(msq_ready, 1)
                    pool.wait_ge(msq_ready, tile * 2 + k + 1)
                    power(msq[:, s], rms[:, s], rms_ready)

                def shift_rows(tile, k):
                    s = slice(2 * k, 2 * k + 2)
                    pool.wait_ge(ys_ready, tile * 2 + k + 1)
                    g.tensor_tensor(xo[:, s, :], xo[:, s, :], vec2[:, s, 2, :], ALU.add).then_inc(y_ready, 1)

                def rounded(dst, src):
                    width = src.shape[-1]
                    by = one[:].broadcast_to([P, width]) if len(src.shape) == 2 else (
                        one[:].unsqueeze(2).broadcast_to([P, src.shape[1], width]))
                    return g.tensor_tensor(dst, src, by, ALU.mult)

                def first_parts(names):
                    for n in names:
                        j = int(n[4:])
                        pool.wait_ge(*gemm.emptied(n, t))
                        rounded(gT[0][:, j, :], whole[:, j % WHOLE, :]).then_inc(g_hi, 1)

                if mlp:
                    scale_and_shift(u, ln2_step, ve2, rs2, nm2, ln2_rstd, ln2_shift)
                if attn:
                    for k, parts in ((2, qparts), (3, kparts)):
                        pool.wait_ge(mid_ready, t * 4 + k + 1)
                        g.tensor_tensor(parts[:, 1, 2, :], whole[:, k, :], parts[:, 1, 1, :], ALU.subtract
                                        ).then_inc(parts_ready, 1)
                if mlp:
                    shift_columns(u, mod2, mod2_in, [(h2_scaled, u * KC + c + 1) for c in range(KC)], hw2, hw2_ready)
                if late:
                    pool.wait_ge(vec2_in, (w + 1) * 32)
                    pool.wait_ge(x1_kept, w + 1)
                    gate_and_add(0, w, misc.emptied("fc2_0", u), mlp_rows, vec2[:, :, 0, :], mlp_gated, xo, xo,
                                 x2_ready)
                    mean_square(w, 0)
                if late:
                    gate_and_add(1, w, misc.emptied("fc2_1", t), mlp_rows, vec2[:, :, 0, :], mlp_gated, xo, xo,
                                 x2_ready)
                    shift_rows(w, 0)
                if mlp:
                    first_parts(fc1_names[0:2])
                if late:
                    mean_square(w, 1)
                if mlp:
                    first_parts(fc1_names[2:4])
                elif attn:
                    pool.wait_ge(mlp_weights_in, 48)
                    for src, (hi, _) in mlp_splits:
                        rounded(hi, src).then_inc(w_hi, 1)
                if late:
                    shift_rows(w, 1)
                if more:
                    next_rstd(t)
                if mlp:
                    first_parts(fc1_names[4:8])
                if more:
                    if mlp:
                        pool.wait_ge(g_ready, u * FC + WHOLE + KC)
                    next_columns(t)
                if attn:
                    pool.wait_ge(x_res_ready, t + 1)
                    if mlp:
                        pool.wait_ge(x1_kept, u + 1)
                    for k in range(2):
                        s = slice(2 * k, 2 * k + 2)
                        pool.wait_ge(attn_gated, t * 2 + k + 1)
                        g.tensor_tensor(x1[:, s, :], x_res[:, s, :], o[:, s, :], ALU.add).then_inc(x1_ready, 1)

            turns(pool, body)


W_SPLITS = 2 * KC + 2
STACK_LOADS = 16 * (len(Q_RUNS) + len(K_RUNS))
PREP_WABS, PREP_SILU, PREP_CQ, PREP_CQT, PREP_TOK, PREP_ALL = 3, 6, 13, 19, 27, 28
ZEROS_ALL = 7
COND_ALL, CONSTS_ALL = 16 * 9, 16 * 8
MOD_COLS = [g * D + k * P for g in (0, 1, 3, 4) for k in range(KC)]


def kernel(x, cond_1024, L0_cond_W_qkv, L0_cond_b_qkv, L0_cond_W_proj, L0_cond_b_proj, L0_cond_W_fc1, L0_cond_b_fc1,
           L0_cond_W_fc2, L0_cond_b_fc2, L0_cond_W_ada, L0_cond_b_ada, L1_cond_w_proj, L1_cond_b_proj,
           L1_cond_rms_weight):
    import numpy as np
    import concourse.bacc as bacc
    from concourse.bass_utils import run_bass_kernel_spmd

    def chunks(w):
        w = np.asarray(w)
        return w.reshape(-1, P, w.shape[1]).transpose(1, 0, 2)

    def columns(b):
        return np.asarray(b).reshape(-1, P).T

    def line(b):
        return np.asarray(b).reshape(1, -1)

    ada_cols = columns(L0_cond_b_ada)
    mod_cols = [m // P for m in MOD_COLS]
    select = np.zeros((P, NI, P), np.float32)
    for a in range(2):
        for i in range(NI):
            for j in range(2):
                select[(a * NI + i) * 2 + j, i, j * SEQ:(j + 1) * SEQ] = 1.0
    arrays = {
        "x": np.asarray(x).reshape(BATCH * SEQ, D),
        "cT": chunks(np.asarray(cond_1024).T),
        "c": cond_1024,
        "w_qkv": chunks(L0_cond_W_qkv),
        "bT_qkv": columns(L0_cond_b_qkv)[:, 0:4],
        "b_v": line(L0_cond_b_qkv)[:, 2 * D:],
        "w_proj": chunks(L0_cond_W_proj),
        "b_proj": line(L0_cond_b_proj),
        "w_fc1": chunks(L0_cond_W_fc1),
        "bT_fc1": columns(L0_cond_b_fc1),
        "w_fc2": chunks(L0_cond_W_fc2),
        "b_fc2": line(L0_cond_b_fc2),
        "w_ada": chunks(L0_cond_W_ada),
        "bT_ada": ada_cols[:, mod_cols],
        "b_ada": line(L0_cond_b_ada),
        "w1T": chunks(np.asarray(L1_cond_w_proj).T),
        "b1": line(L1_cond_b_proj),
        "rms_w": line(L1_cond_rms_weight),
        "ident": np.eye(P, dtype=np.float32),
        "fold": np.tile(np.eye(SEQ, dtype=np.float32), (2, 1)),
        "select": select,
    }
    arrays = {k: np.ascontiguousarray(a) for k, a in arrays.items()}
    nc = bacc.Bacc("TRN2", target_bir_lowering=False, num_devices=1)
    args = {k: nc.dram_tensor(f"in_{k}", a.shape, mybir.dt.from_np(a.dtype), kind="ExternalInput").ap()
            for k, a in arrays.items()}
    result = nc.dram_tensor("out_rows", (BATCH * SEQ, D), F32, kind="ExternalOutput").ap()
    build(nc, out=result, **args)
    r = run_bass_kernel_spmd(nc, [{f"in_{k}": a for k, a in arrays.items()}], core_ids=[0])
    return r.results[0]["out_rows"].reshape(BATCH, SEQ, D)
```

```python
from contextlib import ExitStack

import concourse.bass as bass
from concourse import mybir

F32 = mybir.dt.float32
F32R = mybir.dt.float32r
BF16 = mybir.dt.bfloat16
ALU = mybir.AluOpType
ACT = mybir.ActivationFunctionType
AX = mybir.AxisListType

P = 128
BATCH, SEQ, D = 64, 64, 256
HEADS = 16
HD = D // HEADS
HID = 1024
TOK = 512
NB = TOK // SEQ
TILES = BATCH * SEQ // TOK
NS = TOK // P
KC = D // P
FC = HID // P
PAIRS = HEADS // 2
NI = PAIRS // KC
VW = HD + 1
NPR = 6
Q_RUNS, K_RUNS = ((0, 3, 0, 0), (3, 2, 1, 0), (5, 1, 2, 0)), ((0, 3, 0, 1), (3, 2, 0, 1), (5, 1, 0, 0))
ST = HD * NPR
MAX_ROWS = 3 * HEADS // KC
QK = ("q0", "k0", "q1", "k1")
WHOLE = 4
LN_EPS, RMS_EPS, Q_EPS = 1e-6, 1e-6, 1e-5
ROUND = 1.5 * 2.0**23
SCALE = float(HD) ** -0.5


class Ring:

    def __init__(self, banks, filled, emptied, order, absent):
        self.banks, self.sem_filled, self.sem_emptied = banks, filled, emptied
        self.order, self.absent = order, absent

    def names(self, turn):
        return [n for n in self.order if not n.startswith(self.absent.get(turn, ()))]

    def place(self, name, turn):
        n = len(self.banks)
        if isinstance(turn, int):
            k = sum(len(self.names(before)) for before in range(-1, turn)) + self.names(turn).index(name)
            return k % n, k // n
        k = sum(len(self.names(before)) for before in (-1, 0, 1)) - 2 * len(self.order) + self.order.index(name)
        return k % n, turn * (len(self.order) // n) + k // n

    def bank(self, name, turn):
        return self.banks[self.place(name, turn)[0]]

    def free(self, name, turn):
        b, before = self.place(name, turn)
        return self.sem_emptied[b], before

    def filled(self, name, turn):
        b, before = self.place(name, turn)
        return self.sem_filled[b], before + 1

    def emptied(self, name, turn):
        b, before = self.place(name, turn)
        return self.sem_emptied[b], before + 1

    def signal_filled(self, name, turn):
        return self.sem_filled[self.place(name, turn)[0]], 1

    def signal_emptied(self, name, turn):
        return self.sem_emptied[self.place(name, turn)[0]], 1


def wait(eng, sem, value):
    if isinstance(value, int) and value <= 0:
        return
    eng.wait_ge(sem, value)


def row(ap, t):
    if isinstance(t, int):
        return ap[t]
    return ap[bass.ds(t, 1)].squeeze(0)


def build(nc, x, cT, c, w_qkv, bT_qkv, b_v, w_proj, b_proj, w_fc1, bT_fc1, w_fc2, b_fc2, w_ada, bT_ada,
          b_ada, w1T, b1, rms_w, ident, fold, select, out):
    with ExitStack() as ctx:
        def sb(name, shape, dt=F32):
            return ctx.enter_context(nc.sbuf_tensor(name, shape, dt))

        def sem(name):
            return ctx.enter_context(nc.semaphore(name))

        Wqkv = [sb(f"Wqkv_{n}", [P, KC, 3 * D], F32R) for n in ("hi", "lo")]
        Wp = [sb(f"Wp_{n}", [P, KC, D], F32R) for n in ("hi", "lo")]
        W1 = [sb(f"W1_{n}", [P, KC, HID], F32R) for n in ("hi", "lo")]
        W2 = [sb(f"W2_{n}", [P, FC, D], F32R) for n in ("hi", "lo")]
        bqk = sb("bqk", [P, 4])
        bqk_s = sb("bqk_s", [P, 4])
        b1T = sb("b1T", [P, FC])
        bv = sb("bv", [P, D])
        bp = sb("bp", [P, D])
        b2 = sb("b2", [P, D])
        idn = sb("idn", [P, P])
        fld = sb("fld", [P, SEQ], BF16)
        sel = sb("sel", [P, NI, P], BF16)
        halves = sb("halves", [P, NS])
        epss = sb("epss", [P, NS])
        one = sb("one", [P, 1])
        warm = sb("warm", [P, 1])
        waited = sb("waited", [P, 1])
        badaT = sb("badaT", [P, 8])
        cst = sb("cst", [BATCH, 4])
        wst = sb("wst", [P, 4])
        x_in = sb("x_in", [P, NS, D])
        x_res = sb("x_res", [P, NS, D])
        mod1 = sb("mod1", [P, 4, NB])
        gate1 = sb("gate1", [P, NS, D])
        st1 = sb("st1", [P, NS, 6])
        mv1 = sb("mv1", [P, NS, 2])
        ve1 = sb("ve1", [P, NS])
        rs1 = sb("rs1", [P, NS])
        hn = sb("hn", [P, NS, D])
        hS = sb("hS", [P, KC, TOK])
        hT1 = [sb(f"hT1_{n}", [P, KC, TOK], F32R) for n in ("hi", "lo")]
        whole = sb("whole", [P, WHOLE, TOK])
        qst = sb("qst", [P, HEADS, TOK], BF16)
        kst = sb("kst", [P, HEADS, TOK], BF16)
        v2 = sb("v2", [P, NB, PAIRS, 2, VW])
        nmax = sb("nmax", [P, KC, NI, NB])
        nparts = sb("nparts", [P, KC, 3, NI, NB], BF16)
        nmaxU = sb("nmaxU", [P, KC, NB, 3, NI, 2], BF16)
        pT = sb("pT", [P, PAIRS, TOK])
        rden = sb("rden", [P, NS, HEADS])
        parts = pT[:, 0:6, :].bitcast(BF16).rearrange("p a (x n) -> p (a x) n", x=2)
        qparts = parts[:, 0:6, :].rearrange("p (c a) n -> p c a n", c=KC)
        kparts = parts[:, 6:12, :].rearrange("p (c a) n -> p c a n", c=KC)
        mlp_rows = pT[:, 6:8, :].rearrange("p a (s f) -> p (a s) f", f=D)
        nmaxT = parts[0:MAX_ROWS, 8:8 + KC, :]
        o = hn
        hw1 = whole[:, 0:KC, :]
        hw2 = hn[:].rearrange("p s f -> p (s f)").rearrange("p (k n) -> p k n", k=KC)
        x1 = sb("x1", [P, NS, D])
        mod2 = sb("mod2", [P, 4, NB])
        vec2 = sb("vec2", [P, NS, 3, D])
        st2 = sb("st2", [P, NS, 6])
        mv2 = sb("mv2", [P, NS, 2])
        ve2 = sb("ve2", [P, NS])
        rs2 = sb("rs2", [P, NS])
        nm2 = sb("nm2", [P, NS])
        hT2 = [sb(f"hT2_{n}", [P, KC, TOK], F32R) for n in ("hi", "lo")]
        gT = [sb(f"gT_{n}", [P, FC, TOK], F32R) for n in ("hi", "lo")]
        oT = hT2
        xo = sb("xo", [P, NS, D])
        ssq = sb("ssq", [P, NS])
        msq = sb("msq", [P, NS])
        rms = sb("rms", [P, NS])
        Wada = qst[:, 0:12, :].bitcast(F32).rearrange("p a b -> p (a b)").rearrange("p (k n) -> p k n", k=KC)
        Wc, Wcq = pT[:, 0:KC, :], pT[:, KC:2 * KC, :]
        sel32, fld32 = pT[:, 4, :].rearrange("p (i q) -> p i q", i=NI), pT[:, 7, D:D + SEQ]
        emb, bc, rmsw = pT[0:BATCH, 5, :], pT[0:BATCH, 6, :], pT[0:BATCH, 7, 0:D]
        tok_vec = o[0:BATCH, :, :]
        cTs, sil, sg, cqT = (whole[:, 3, k * P:(k + 1) * P].rearrange("p (k b) -> p k b", k=KC) for k in range(4))
        ones = x_res[:, 0, 0:P]
        mod_all = whole[:, 2, :].rearrange("p (t v b) -> p t v b", t=TILES, v=8)
        bada, cb, cq = x1[0:BATCH, 0:2, :], x1[0:BATCH, 2, :], x1[0:BATCH, 3, :]
        Wqkv32 = kst[:, 0:6, :].bitcast(F32).rearrange("p a b -> p (a b)").rearrange("p (k n) -> p k n", k=KC)
        Wp32 = kst[:, 6:8, :].bitcast(F32)
        flat = vec2[:].rearrange("p s v f -> p (s v f)")
        W1_32 = flat[:, 0:KC * HID].rearrange("p (k n) -> p k n", k=KC)
        W2_32 = [flat[:, KC * HID:].rearrange("p (k n) -> p k n", n=D), xo]
        scr = nc.dram_tensor("scr", (BATCH, 4, D), F32, kind="Internal").ap()
        scr_mod = nc.dram_tensor("scr_mod", (P, TILES, 8, NB), F32, kind="Internal").ap()
        scr_qk = [[nc.dram_tensor(f"scr_{n}{c}", (3, HD, HEADS // KC, TOK), BF16, kind="Internal").ap() for n in "qk"]
                  for c in range(KC)]
        lg = ctx.enter_context(nc.psum_tensor("lg", [P, NI, TOK], F32))
        gb = [ctx.enter_context(nc.psum_tensor(f"gb{i}", [P, TOK], F32)) for i in range(2)]
        tb = [ctx.enter_context(nc.psum_tensor(f"tb{i}", [P, TOK], F32)) for i in range(2)]

        fc1_names = [f"fc1_{j}" for j in range(FC)]
        gemm = Ring(gb, [sem(f"gemm_filled{i}") for i in range(2)], [sem(f"gemm_emptied{i}") for i in range(2)],
                    ["q0", "k0", "q1", "k1", "v0", "v1", *fc1_names, "oT0", "oT1", "proj0", "proj1"],
                    {-1: ("",), 0: ("fc",), TILES: ("q", "k", "v", "oT", "proj")})
        misc = Ring(tb, [sem(f"misc_filled{i}") for i in range(2)], [sem(f"misc_emptied{i}") for i in range(2)],
                    ["fc2_1", "max0", "max1", "h1_0", "h1_1", "fc2_0"],
                    {-1: ("fc", "max"), 0: ("fc",), 1: ("fc2_1",), TILES - 1: ("h1",), TILES: ("max", "h1")})
        logit = Ring([lg], [sem("logits_filled")], [sem("logits_emptied")], ["s0", "s1", "sT0", "sT1", "pv"],
                     {-1: ("",), TILES: ("s", "pv")})

        consts_in = sem("consts_in")
        cT_in = sem("cT_in")
        quant_in = sem("quant_in")
        ident_in = sem("ident_in")
        ada_in = sem("ada_in")
        cond_in = sem("cond_in")
        weights_in = sem("weights_in")
        mlp_weights_in = sem("mlp_weights_in")
        prep = sem("prep")
        prep_act = sem("prep_act")
        prep_pe = sem("prep_pe")
        zeros_set = sem("zeros_set")
        mods_out = sem("mods_out")
        scratch_out = sem("scratch_out")
        x_in_ready = sem("x_in_ready")
        mod1_in = sem("mod1_in")
        gate1_in = sem("gate1_in")
        mod2_in = sem("mod2_in")
        vec2_in = sem("vec2_in")
        x_res_ready = sem("x_res_ready")
        ln1_step = sem("ln1_step")
        ln1_rstd = sem("ln1_rstd")
        hn1_ready = sem("hn1_ready")
        hw1_ready = sem("hw1_ready")
        hT1_hi = sem("hT1_hi")
        oT_hi = sem("oT_hi")
        hT1_ready = sem("hT1_ready")
        parts_step = sem("parts_step")
        parts_ready = sem("parts_ready")
        parts_out = [[sem(f"part{a}_out_{n}") for a in range(3)] for n in QK]
        stacks_in = [sem(f"stacks_in{c}") for c in range(KC)]
        nmax_step = sem("nmax_step")
        nmaxU_ready = sem("nmaxU_ready")
        rden_ready = sem("rden_ready")
        attn_gated = sem("attn_gated")
        x1_ready = sem("x1_ready")
        ln2_step = sem("ln2_step")
        ln2_rstd = sem("ln2_rstd")
        ln2_shift = sem("ln2_shift")
        hn2_ready = sem("hn2_ready")
        h2_filled = sem("h2_filled")
        h2_scaled = sem("h2_scaled")
        hw2_ready = sem("hw2_ready")
        hT2_hi = sem("hT2_hi")
        hT2_ready = sem("hT2_ready")
        g_hi = sem("g_hi")
        g_ready = sem("g_ready")
        w_hi = sem("w_hi")
        w_ready = sem("w_ready")
        x1_kept = sem("x1_kept")
        mlp_gated = sem("mlp_gated")
        high_ready = sem("high_ready")
        mid_ready = sem("mid_ready")
        x2_ready = sem("x2_ready")
        ssq_ready = sem("ssq_ready")
        msq_ready = sem("msq_ready")
        rms_ready = sem("rms_ready")
        ys_ready = sem("ys_ready")
        y_ready = sem("y_ready")
        y_stored = [sem(f"y_stored{k}") for k in range(2)]

        block = ctx.enter_context(nc.Block())

        def turns(eng, body):
            body(0, attn=True, mlp=False, late=False, more=True)
            body(1, attn=True, mlp=True, late=False, more=True)
            with eng.Fori(2, TILES - 1) as t:
                body(t, attn=True, mlp=True, late=True, more=True)
            body(TILES - 1, attn=True, mlp=True, late=True, more=False)
            body(TILES, attn=False, mlp=True, late=True, more=False)
            body(TILES + 1, attn=False, mlp=False, late=True, more=False)

        mlp_splits = [(W1_32[:, k, :], (W1[0][:, k, :], W1[1][:, k, :])) for k in range(KC)] + [
            (W2_32[k][:], (W2[0][:, k * FC // 2:(k + 1) * FC // 2, :], W2[1][:, k * FC // 2:(k + 1) * FC // 2, :]))
            for k in range(2)]

        x_v = x.rearrange("(t s p) f -> t p s f", s=NS, p=P)
        out_v = out.rearrange("(t s p) f -> t p s f", s=NS, p=P)
        scr_v = scr.rearrange("(t s h) v f -> t h s v f", s=NS, h=2)

        def mods(t, v):
            if isinstance(t, int):
                return scr_mod[:, t, v:v + 4, :]
            return scr_mod[:, bass.ds(t, 1), v:v + 4, :].squeeze(1)

        @block.sync
        def _(sp):
            sp.dma_start(cTs[:], cT).then_inc(cT_in, 16)
            for dst, src in ((Wc, w1T), (cb, c)):
                sp.dma_start(dst[:], src).then_inc(quant_in, 16)
            sp.dma_start(x_in[:], x_v[0]).then_inc(x_in_ready, 16)
            sp.dma_start(idn[:], ident).then_inc(ident_in, 16)
            for dst, src in ((Wada, w_ada), (badaT, bT_ada)):
                sp.dma_start(dst[:], src).then_inc(ada_in, 16)
            sp.dma_start(Wqkv32[:], w_qkv).then_inc(weights_in, 16)
            for k, g in enumerate((2, 5)):
                sp.dma_start(bada[:, k, :], b_ada[:, g * D:(g + 1) * D].partition_broadcast(BATCH).rearrange(
                    "p a f -> p (a f)")).then_inc(cond_in, 16)
            for dst, src in ((bc, b1), (rmsw, rms_w)):
                sp.dma_start(dst[:], src.partition_broadcast(BATCH).rearrange("p a f -> p (a f)")).then_inc(cond_in, 16)
            for dst, src in ((fld32, fold), (sel32, select), (bqk, bT_qkv), (b1T, bT_fc1)):
                sp.dma_start(dst[:], src).then_inc(consts_in, 16)
            for dst, src in ((bv, b_v), (bp, b_proj), (b2, b_fc2)):
                sp.dma_start(dst[:], src.partition_broadcast(P).rearrange("p a f -> p (a f)")).then_inc(consts_in, 16)
            sp.dma_start(Wp32, w_proj).then_inc(weights_in, 16)
            sp.dma_start(W1_32[:], w_fc1).then_inc(mlp_weights_in, 16)
            for k, half in enumerate(W2_32):
                sp.dma_start(half[:], w_fc2[:, k * FC // 2:(k + 1) * FC // 2, :]).then_inc(mlp_weights_in, 16)
            sp.wait_ge(prep, PREP_MODS)
            sp.dma_start(scr_mod, mod_all).then_inc(mods_out, 16)
            sp.wait_ge(prep, PREP_TOK)
            sp.dma_start(scr, tok_vec[:]).then_inc(scratch_out, 16)

            def store(tile, k):
                sp.wait_ge(y_ready, tile * 2 + k + 1)
                sp.dma_start(row(out_v, tile)[:, 2 * k:2 * k + 2, :], xo[:, 2 * k:2 * k + 2, :]
                             ).then_inc(y_stored[k], 16)

            def write_part(t, n, a):
                k, c = QK.index(n), int(n[1])
                sp.wait_ge((high_ready, mid_ready, parts_ready)[a], t * 4 + k + 1)
                sp.dma_start(scr_qk[c]["qk".index(n[0])][a].rearrange("d h n -> h d n"),
                             (kparts if n[0] == "k" else qparts)[:, c, a, :]).then_inc(parts_out[k][a], 16)

            def read_stacks(t, c, a):
                for n, (stack, (first, blocks, part, step)) in enumerate(((qst, Q_RUNS[a]), (kst, K_RUNS[2 - a]))):
                    for written in range(part, part + (blocks if step else 1)):
                        sp.wait_ge(parts_out[2 * c + n][written], (t + 1) * 16)
                    if step:
                        src = scr_qk[c][n][part:part + blocks].rearrange("a d h n -> (a d) (h n)")
                    else:
                        src = scr_qk[c][n][part:part + 1].rearrange("a d h n -> a d (h n)").broadcast_to(
                            [blocks, HD, TOK * HEADS // KC])
                    sp.dma_start(stack[first * HD:(first + blocks) * HD, c * HEADS // KC:(c + 1) * HEADS // KC, :],
                                 src).then_inc(stacks_in[c], 16)

            def body(t, attn, mlp, late, more):
                u, w = t - 1, t - 2
                if mlp:
                    wait(sp, hT2_ready, u * KC)
                    sp.dma_start(mod2[:], mods(u, 4)).then_inc(mod2_in, 16)
                if attn:
                    if not (isinstance(t, int) and t == 0):
                        sp.wait_ge(*logit.filled("sT1", u))
                    for c in range(KC):
                        for a in range(3):
                            write_part(t, f"q{c}", a)
                            write_part(t, f"k{c}", a)
                        for a in range(3):
                            read_stacks(t, c, a)
                if not mlp and attn:
                    sp.wait_ge(mods_out, 16)
                    sp.wait_ge(scratch_out, 16)
                    for h in range(2):
                        sp.dma_start(gate1[h * SEQ:(h + 1) * SEQ, :, :], scr_v[0, h, :, 0, :].partition_broadcast(SEQ)
                                     ).then_inc(gate1_in, 16)
                if more:
                    sp.wait_ge(hn1_ready, (t + 1) * NS)
                    sp.wait_ge(x_res_ready, t + 1)
                    sp.dma_start(x_in[:], row(x_v, t + 1)).then_inc(x_in_ready, 16)
                    sp.wait_ge(hT1_ready, (t + 1) * KC)
                    sp.dma_start(mod1[:], mods(t + 1, 0)).then_inc(mod1_in, 16)
                if late:
                    store(w, 0)
                if mlp and attn:
                    sp.wait_ge(attn_gated, t * 2)
                    for h in range(2):
                        sp.dma_start(gate1[h * SEQ:(h + 1) * SEQ, :, :],
                                     row(scr_v, t)[h, :, 0, :].partition_broadcast(SEQ)).then_inc(gate1_in, 16)
                if late:
                    store(w, 1)
                if mlp:
                    if isinstance(u, int) and u == 0:
                        sp.wait_ge(w_ready, W_SPLITS)
                    for h in range(2):
                        sp.dma_start(vec2[h * SEQ:(h + 1) * SEQ, :, :, :],
                                     row(scr_v, u)[h, :, 1:4, :].partition_broadcast(SEQ)).then_inc(vec2_in, 16)

            turns(sp, body)
            sp.wait_ge(y_stored[0], 16 * TILES)
            sp.wait_ge(y_stored[1], 16 * TILES)

        @block.tensor
        def _(pe):
            mm = nc.tensor.matmul
            pe.wait_ge(prep, PREP_WABS)
            mm(lg[:, 1, 0:2], ones[:], wst[:, 0:2], start=True, stop=True).then_inc(prep_pe, 1)
            pe.wait_ge(ada_in, 32)
            for n, col in enumerate(MOD_COLS):
                for k in range(KC):
                    last = mm(gb[0][:, n * BATCH:(n + 1) * BATCH], Wada[:, k, col:col + P], sil[:, k, :],
                              start=(k == 0), stop=(k == KC - 1))
            last.then_inc(prep_pe, 1)

            def transpose(dst, src, c):
                for s in range(NS):
                    last = nc.tensor.transpose(dst[:, s * P:(s + 1) * P], src[:, s, c * P:(c + 1) * P], idn[:])
                return last

            def to_features(ring, name, t, src):
                wait(pe, *ring.free(name, t))
                transpose(ring.bank(name, t), src, int(name[-1])).then_inc(*ring.signal_filled(name, t))

            def product(dst, stationary, moving, chunks, there=None, part=None):
                pairs = ((0, 0), (0, 1), (1, 0))
                for k in range(chunks) if part is None else part:
                    if there is not None:
                        pe.wait_ge(there[0], there[1] + k + 1)
                    for n, (a, b) in enumerate(pairs):
                        last = mm(dst, stationary(a, k), moving(b, k), start=(k == 0 and n == 0),
                                  stop=(k == chunks - 1 and n == len(pairs) - 1))
                return last

            def columns_out(name, t, w, col, src):
                wait(pe, *gemm.free(name, t))
                product(gemm.bank(name, t)[:], lambda a, k: w[a][:, k, col:col + P], lambda b, k: src[b][:, k, :], KC
                        ).then_inc(*gemm.signal_filled(name, t))

            def fc1(names, t):
                for n in names:
                    columns_out(n, t, W1, int(n[4:]) * P, hT2)

            def rows_out(ring, name, t, src, w, col, chunks):
                for s in range(2):
                    block_out(ring, name, t, s, src, w, col, chunks)

            def block_out(ring, name, t, s, src, w, col, chunks, there=None, part=None):
                part = range(chunks) if part is None else part
                if s == 0 and part[0] == 0:
                    wait(pe, *ring.free(name, t))
                tok = (2 * int(name[-1]) + s) * P
                last = product(ring.bank(name, t)[:, s * D:(s + 1) * D], lambda a, k: src[a][:, k, tok:tok + P],
                               lambda b, k: w[b][:, k, col:col + D], chunks, there, part)
                if s == 1 and part[-1] == chunks - 1:
                    last.then_inc(*ring.signal_filled(name, t))

            def logits(name, t):
                c = int(name[-1])
                st = name.startswith("sT")
                wait(pe, *logit.free(name, t))
                if st:
                    pe.wait_ge(*misc.emptied(f"max{c}", t))
                    for i in range(NI):
                        mm(lg[:, i, :], sel[0:MAX_ROWS, i, :], nmaxT[:, c, :], start=True, stop=False,
                           skip_group_check=True)
                stat, mov = (kst, qst) if st else (qst, kst)
                for j in range(2):
                    for b in range(NB):
                        tk = slice(b * SEQ, (b + 1) * SEQ)
                        for i in range(NI):
                            head = 2 * (c * NI + i) + j
                            last = mm(lg[j * SEQ:(j + 1) * SEQ, i, tk], stat[0:ST, head, tk], mov[0:ST, head, tk],
                                      start=(not st), stop=True, skip_group_check=True)
                last.then_inc(*logit.signal_filled(name, t))

            def turn_max(c, t):
                n = f"max{c}"
                pe.wait_ge(nmaxU_ready, t * KC + c + 1)
                wait(pe, *misc.free(n, t))
                for b in range(NB):
                    last = mm(misc.bank(n, t)[0:MAX_ROWS, b * SEQ:(b + 1) * SEQ],
                              nmaxU[:, c, b, :, :, :].rearrange("p a i j -> p (a i j)"), fld[:],
                              start=True, stop=True)
                last.then_inc(*misc.signal_filled(n, t))

            def rows_of_next(turn):
                pe.wait_ge(hn1_ready, (turn + 2) * NS)
                to_features(misc, "h1_0", turn, hn)
                to_features(misc, "h1_1", turn, hn)

            pe.wait_ge(ident_in, 16)
            rows_of_next(-1)
            pe.wait_ge(prep, PREP_CQ)
            for k in range(KC):
                last = nc.tensor.transpose(lg[:, 2, k * BATCH:(k + 1) * BATCH], cq[:, k * P:(k + 1) * P],
                                           idn[0:BATCH, 0:BATCH])
            last.then_inc(prep_pe, 1)
            for n, g in enumerate((2, 5)):
                for k in range(KC):
                    last = mm(gb[1][0:BATCH, n * D:(n + 1) * D], sil[:, k, :], Wada[:, k, g * D:(g + 1) * D],
                              start=(k == 0), stop=(k == KC - 1))
            last.then_inc(prep_pe, 1)
            pe.wait_ge(prep, PREP_CQT)
            for k in range(KC):
                last = mm(lg[0:BATCH, 0, :], cqT[:, k, :], Wcq[:, k, :], start=(k == 0), stop=(k == KC - 1))
            last.then_inc(prep_pe, 1)
            pe.wait_ge(prep, PREP_GATES)
            pe.wait_ge(zeros_set, ZEROS_ALL)

            def body(t, attn, mlp, late, more):
                u = t - 1

                def fc2_first(s, part):
                    block_out(misc, "fc2_0", t, s, gT, W2, 0, FC, (g_ready, u * FC) if s == 0 else None, part)

                if attn:
                    pe.wait_ge(hT1_ready, (t + 1) * KC)
                    for n in QK:
                        columns_out(n, t, Wqkv, (D if n[0] == "k" else 0) + int(n[1]) * P, hT1)
                    rows_out(gemm, "v0", t, hT1, Wqkv, 2 * D, KC)
                    rows_out(gemm, "v1", t, hT1, Wqkv, 2 * D, KC)
                if late:
                    block_out(misc, "fc2_1", t, 0, gT, W2, 0, FC)
                if mlp:
                    pe.wait_ge(hn2_ready, (u + 1) * NS)
                    for c in range(KC):
                        last = transpose(lg[:, c, :], hn, c)
                    last.then_inc(h2_filled, 1)
                if late:
                    block_out(misc, "fc2_1", t, 1, gT, W2, 0, FC)
                if attn:
                    if mlp:
                        pe.wait_ge(h2_scaled, (u + 1) * KC)
                    else:
                        pe.wait_ge(prep, PREP_ALL)
                    pe.wait_ge(stacks_in[0], (t + 1) * STACK_LOADS)
                    logits("s0", t)
                if mlp:
                    pe.wait_ge(w_ready, W_SPLITS)
                    pe.wait_ge(hT2_ready, (u + 1) * KC)
                    fc1(fc1_names[0:4], t)
                if attn:
                    pe.wait_ge(stacks_in[1], (t + 1) * STACK_LOADS)
                    logits("s1", t)
                    turn_max(0, t)
                if mlp:
                    fc1(fc1_names[4:6], t)
                if attn:
                    logits("sT0", t)
                    turn_max(1, t)
                if mlp:
                    fc1(fc1_names[6:7], t)
                if attn:
                    logits("sT1", t)
                if more:
                    rows_of_next(t)
                if mlp:
                    fc1(fc1_names[7:8], t)
                if attn:
                    pe.wait_ge(*gemm.emptied("v0", t))
                    pe.wait_ge(*gemm.emptied("v1", t))
                    wait(pe, *logit.free("pv", t))
                    for b in range(NB):
                        half = slice(b % 2 * SEQ, (b % 2 + 1) * SEQ)
                        for p in range(PAIRS):
                            last = mm(lg[half, b // 2, p * 2 * VW:(p + 1) * 2 * VW], pT[:, p, b * SEQ:(b + 1) * SEQ],
                                      v2[:, b, p, :, :].rearrange("p j e -> p (j e)"), start=True, stop=True)
                        if b == NB - 1:
                            last.then_inc(*logit.signal_filled("pv", t))
                        if mlp and b % 2 == 1:
                            fc2_first(0, range(b // 2, b // 2 + 1))
                if mlp:
                    fc2_first(0, range(NB // 2 if attn else 0, FC))
                if mlp and attn:
                    fc2_first(1, range(0, FC // 4))
                if attn:
                    pe.wait_ge(*logit.emptied("pv", t))
                    to_features(gemm, "oT0", t, o)
                    to_features(gemm, "oT1", t, o)
                if mlp:
                    fc2_first(1, range(FC // 4 if attn else 0, FC))
                if attn:
                    pe.wait_ge(*gemm.emptied("oT0", t))
                    pe.wait_ge(*gemm.emptied("oT1", t))
                    rows_out(gemm, "proj0", t, oT, Wp, 0, KC)
                    rows_out(gemm, "proj1", t, oT, Wp, 0, KC)

            turns(pe, body)

        @block.scalar
        def _(act):
            act.wait_ge(cT_in, 16)
            nc.scalar.activation(sg[:], cTs[:], ACT.Exp, scale=-1.0).then_inc(prep_act, 1)
            act.wait_ge(consts_in, CONSTS_ALL)
            nc.scalar.mul(bqk_s[:], bqk[:], SCALE).then_inc(prep_act, 1)
            act.wait_ge(prep_act, 2)

            def squares(tile, k):
                act.wait_ge(x2_ready, tile * 2 + k + 1)
                for s in (2 * k, 2 * k + 1):
                    nc.scalar.activation(mlp_rows[:, s, :], xo[:, s, :], ACT.Square, scale=float(D) ** -0.5,
                                         accum_out=ssq[:, s:s + 1]).then_inc(ssq_ready, 1)

            def normalised(t):
                act.wait_ge(ln2_shift, t + 1)
                for s in (0, 1):
                    nc.scalar.activation(hn[:, s, :], x1[:, s, :], ACT.Identity, bias=nm2[:, s:s + 1],
                                         scale=rs2[:, s:s + 1]).then_inc(hn2_ready, 1)

            act.wait_ge(zeros_set, ZEROS_ALL)
            act.wait_ge(mods_out, 16)
            act.wait_ge(prep, PREP_ALL)

            def body(t, attn, mlp, late, more):
                u, w = t - 1, t - 2

                def queries_keys(n):
                    c = int(n[1])
                    act.wait_ge(*gemm.filled(n, t))
                    k = QK.index(n)
                    if n[0] == "q":
                        ins = nc.scalar.activation(whole[:, k, :], gemm.bank(n, t)[:], ACT.Identity,
                                                   bias=bqk_s[:, c:c + 1], scale=SCALE)
                    else:
                        ins = nc.scalar.activation(whole[:, k, :], gemm.bank(n, t)[:], ACT.Identity,
                                                   bias=bqk[:, KC + c:KC + c + 1])
                    ins.then_inc(*gemm.signal_emptied(n, t))
                    act.wait_ge(*gemm.emptied(n, t))
                    nc.scalar.copy((kparts if n[0] == "k" else qparts)[:, c, 0, :], whole[:, k, :]
                                   ).then_inc(high_ready, 1)

                def max_rows():
                    act.wait_ge(*misc.filled("max0", t))
                    nc.scalar.copy(nmaxT[:, 0, :], misc.bank("max0", t)[0:MAX_ROWS, :]
                                   ).then_inc(*misc.signal_emptied("max0", t))

                def probabilities(c):
                    act.wait_ge(*logit.filled(f"sT{c}", t))
                    nc.scalar.activation(pT[:, c * NI:(c + 1) * NI, :], lg[:], ACT.Exp
                                         ).then_inc(*logit.signal_emptied(f"sT{c}", t))

                def gelu(names):
                    for n in names:
                        j = int(n[4:])
                        if j >= WHOLE:
                            act.wait_ge(g_ready, u * FC + j - WHOLE + 1)
                        elif attn:
                            act.wait_ge(parts_ready, t * 4 + j + 1)
                        act.wait_ge(*gemm.filled(n, t))
                        nc.scalar.activation(whole[:, j % WHOLE, :], gemm.bank(n, t)[:], ACT.Gelu_apprx_tanh,
                                             bias=b1T[:, j:j + 1]).then_inc(*gemm.signal_emptied(n, t))

                if attn:
                    queries_keys("q0")
                    queries_keys("k0")
                    queries_keys("q1")
                    queries_keys("k1")
                    wait(act, x1_ready, t * 2)
                    act.wait_ge(x_in_ready, (t + 1) * 16)
                    nc.scalar.copy(x_res[:], x_in[:]).then_inc(x_res_ready, 1)
                if mlp:
                    normalised(u)
                if late:
                    squares(w, 0)
                if mlp:
                    gelu(fc1_names[0:2])
                if late:
                    squares(w, 1)
                if mlp:
                    gelu(fc1_names[2:4])
                if attn:
                    max_rows()
                if mlp:
                    gelu(fc1_names[4:6])
                if attn:
                    nc.scalar.activation(warm[:], halves[:, 0:1], ACT.Exp)
                    probabilities(0)
                    probabilities(1)
                if mlp:
                    gelu(fc1_names[6:8])
                    for k in range(2):
                        wait(act, y_stored[k], u * 16)
                    nc.scalar.copy(xo[:], x1[:]).then_inc(x1_kept, 1)
                if attn:
                    for c in range(KC):
                        act.wait_ge(*gemm.filled(f"oT{c}", t))
                        nc.scalar.copy(oT[0][:, c, :], gemm.bank(f"oT{c}", t)[:]).then_inc(oT_hi, 1)

            turns(act, body)

        @block.vector
        def _(dve):
            v = nc.vector
            steps = [0]

            def link(ins):
                steps[0] += 1
                ins.then_inc(prep, 1)
                dve.wait_ge(prep, steps[0])

            v.memset(v2[:], 0.0).then_inc(zeros_set, 1)
            v.memset(nmaxU[:], 0.0).then_inc(zeros_set, 1)
            v.memset(halves[:], -0.5).then_inc(zeros_set, 1)
            v.memset(epss[:], RMS_EPS).then_inc(zeros_set, 1)
            v.memset(one[:], 1.0).then_inc(zeros_set, 1)
            dve.wait_ge(zeros_set, 5)
            v.memset(v2[0:SEQ, :, :, 0, HD:VW], 1.0).then_inc(zeros_set, 1)
            v.memset(v2[SEQ:P, :, :, 1, HD:VW], 1.0).then_inc(zeros_set, 1)
            link(v.memset(wst[:], 0.0))
            link(v.memset(ones[:], 1.0))
            def statistics(t, src, st, mv, ve, nm, step):
                for s in range(NS):
                    last = v.bn_stats(st[:, s, :], src[:, s, :])
                last.then_inc(step, 1)
                dve.wait_ge(step, t * 3 + 1)
                v.memset(waited[:], 0.0)
                for s in range(NS):
                    last = v.bn_aggr(mv[:, s, :], st[:, s, :])
                last.then_inc(step, 1)
                dve.wait_ge(step, t * 3 + 2)
                if nm is not None:
                    v.tensor_scalar(nm[:], mv[:, :, 0], -1.0, None, ALU.mult)
                v.tensor_scalar(ve[:], mv[:, :, 1], LN_EPS, None, ALU.add).then_inc(step, 1)

            def columns(banks, mod, dst, his):
                for c, (bank, filled, emptied, _) in enumerate(banks):
                    dve.wait_ge(*filled)
                    v.tensor_tensor(hS[:, c, :].rearrange("p (b n) -> p b n", b=NB),
                                    bank.rearrange("p (b n) -> p b n", b=NB),
                                    mod[:, KC + c, :].unsqueeze(2).broadcast_to([P, NB, SEQ]), ALU.mult
                                    ).then_inc(*emptied)
                for c, (*_, scaled) in enumerate(banks):
                    dve.wait_ge(*scaled)
                    v.tensor_tensor(dst[0][:, c, :].rearrange("p (b n) -> p b n", b=NB),
                                    hS[:, c, :].rearrange("p (b n) -> p b n", b=NB),
                                    mod[:, c, :].unsqueeze(2).broadcast_to([P, NB, SEQ]), ALU.add).then_inc(his, 1)

            def columns_rest(tile, dst, his, hw, whole_ready, ready):
                dve.wait_ge(his, (tile + 1) * KC)
                for c in range(KC):
                    dve.wait_ge(whole_ready, tile * KC + c + 1)
                    v.tensor_tensor(dst[1][:, c, :], hw[:, c, :], dst[0][:, c, :], ALU.subtract).then_inc(ready, 1)

            def rows_in(ring, name, t, bias, dst):
                dve.wait_ge(*ring.filled(name, t))
                v.tensor_tensor(dst, ring.bank(name, t)[:].rearrange("p (s f) -> p s f", s=2),
                                bias[:].unsqueeze(1).broadcast_to([P, 2, D]), ALU.add
                                ).then_inc(*ring.signal_emptied(name, t))

            def ln1(t):
                dve.wait_ge(x_in_ready, (t + 1) * 16)
                statistics(t, x_in, st1, mv1, ve1, None, ln1_step)

            def normalised(t, blocks, src, mv, rs, rstd, ready):
                dve.wait_ge(rstd, t + 1)
                for s in blocks:
                    v.tensor_scalar(hn[:, s, :], src[:, s, :], mv[:, s, 0:1], rs[:, s:s + 1], ALU.subtract, ALU.mult
                                    ).then_inc(ready, 1)

            def ln1_rows(t):
                normalised(t, range(NS), x_in, mv1, rs1, ln1_rstd, hn1_ready)

            def columns_of_next(turn):
                dve.wait_ge(mod1_in, (turn + 2) * 16)
                columns([(misc.bank(n, turn)[:], misc.filled(n, turn), misc.signal_emptied(n, turn),
                          misc.emptied(n, turn)) for n in ("h1_0", "h1_1")], mod1, hT1, hT1_hi)

            def columns_of_next_rest(turn):
                columns_rest(turn + 1, hT1, hT1_hi, hw1, hw1_ready, hT1_ready)

            dve.wait_ge(prep_act, 1)
            link(v.tensor_scalar(sil[:], sg[:], 1.0, None, ALU.add))
            link(v.reciprocal(sg[:], sil[:]))
            link(v.tensor_tensor(sil[:], cTs[:], sg[:], ALU.mult))
            dve.wait_ge(quant_in, 32)
            link(v.tensor_reduce(wst[:, 0:1], Wc[:].rearrange("p k n -> p (k n)"), AX.X, ALU.add,
                                 apply_absolute_value=True))
            assert steps[0] == PREP_WABS
            link(v.tensor_reduce(cst[:, 0:1], cb[:], AX.X, ALU.max, apply_absolute_value=True))
            link(v.tensor_scalar(cst[:, 0:1], cst[:, 0:1], Q_EPS, None, ALU.max))
            link(v.reciprocal(cst[:, 1:2], cst[:, 0:1]))
            link(v.tensor_scalar(cst[:, 1:2], cst[:, 1:2], 127.0, None, ALU.mult))
            link(v.tensor_scalar(cq[:], cb[:], cst[:, 1:2], ROUND, ALU.mult, ALU.add))
            link(v.tensor_scalar(cq[:], cq[:], ROUND, 127.0, ALU.subtract, ALU.min))
            link(v.tensor_scalar(cq[:], cq[:], -128.0, None, ALU.max))
            assert steps[0] == PREP_CQ
            ln1(0)
            dve.wait_ge(prep_pe, 1)
            link(v.tensor_scalar(wst[:, 2:3], lg[:, 1, 0:1], 1.0 / (2 * D * D), Q_EPS, ALU.mult, ALU.max))
            link(v.reciprocal(wst[:, 3:4], wst[:, 2:3]))
            link(v.tensor_scalar(Wcq[:], Wc[:], wst[:, 3:4], ROUND, ALU.mult, ALU.add))
            link(v.tensor_scalar(Wcq[:], Wcq[:], ROUND, 1.0, ALU.subtract, ALU.min))
            link(v.tensor_scalar(Wcq[:], Wcq[:], -1.0, None, ALU.max))
            ln1_rows(0)
            dve.wait_ge(weights_in, 32)
            for k in range(KC):
                v.tensor_copy(Wqkv[0][:, k, :], Wqkv32[:, k, :]).then_inc(w_hi, 1)
            v.tensor_copy(Wp[0][:], Wp32).then_inc(w_hi, 1)
            for k in range(KC):
                dve.wait_ge(w_hi, k + 1)
                v.tensor_tensor(Wqkv[1][:, k, :], Wqkv32[:, k, :], Wqkv[0][:, k, :], ALU.subtract
                                ).then_inc(w_ready, 1)
            dve.wait_ge(w_hi, KC + 1)
            v.tensor_tensor(Wp[1][:], Wp32, Wp[0][:], ALU.subtract).then_inc(w_ready, 1)
            dve.wait_ge(prep_pe, 2)
            link(v.tensor_tensor(mod_all[:].rearrange("p t v b -> p v t b"),
                                 gb[0][:].rearrange("p (v t b) -> p v t b", v=8, t=TILES),
                                 badaT[:].unsqueeze(2).unsqueeze(3).broadcast_to([P, 8, TILES, NB]), ALU.add))
            scales = mod_all[:].rearrange("p t (w z) b -> p w t (z b)", w=4)
            for w in (1, 3):
                link(v.tensor_scalar(scales[:, w, :, :], scales[:, w, :, :], 1.0, None, ALU.add))
            assert steps[0] == PREP_MODS
            v.tensor_copy(mod1[:], mod_all[:, 0, 0:4, :]).then_inc(mod1_in, 16)
            columns_of_next(-1)
            dve.wait_ge(prep_pe, 3)
            link(v.tensor_copy(cqT[:].rearrange("p k b -> p (k b)"), lg[:, 2, 0:KC * BATCH]))
            assert steps[0] == PREP_CQT
            columns_of_next_rest(-1)
            dve.wait_ge(cond_in, COND_ALL)
            dve.wait_ge(prep_pe, 4)
            link(v.tensor_tensor(tok_vec[:, 0:2, :], gb[1][0:BATCH, :].rearrange("p (v f) -> p v f", v=2), bada[:],
                                 ALU.add))
            assert steps[0] == PREP_GATES
            link(v.tensor_scalar(cst[:, 2:3], cst[:, 0:1], 1.0 / 127.0, wst[0:BATCH, 2:3], ALU.mult, ALU.mult))
            dve.wait_ge(consts_in, CONSTS_ALL)
            link(v.tensor_copy(sel[:], sel32[:]))
            link(v.tensor_copy(fld[:], fld32))
            dve.wait_ge(prep_pe, 5)
            link(v.scalar_tensor_tensor(emb[:], lg[0:BATCH, 0, :], cst[:, 2:3], bc[:], ALU.mult, ALU.add))
            link(v.scalar_tensor_tensor(tok_vec[:, 2, :], emb[:, 0:D], 1.0, rmsw[:], ALU.add, ALU.mult))
            link(v.tensor_copy(tok_vec[:, 3, :], emb[:, D:2 * D]))
            assert steps[0] == PREP_TOK == PREP_ALL

            def body(t, attn, mlp, late, more):
                u, w = t - 1, t - 2

                def split(n):
                    c, k = int(n[1]), QK.index(n)
                    left, dst = whole[:, k, :], (kparts if n[0] == "k" else qparts)[:, c, :, :]
                    dve.wait_ge(high_ready, t * 4 + k + 1)
                    v.tensor_tensor(left, left, dst[:, 0, :], ALU.subtract).then_inc(parts_step, 1)
                    dve.wait_ge(parts_step, t * 4 + k + 1)
                    v.tensor_copy(dst[:, 1, :], left).then_inc(mid_ready, 1)

                def attended():
                    heads = lg[:, :, 0:HEADS * VW].rearrange("p s (h e) -> p s h e", e=VW)
                    dve.wait_ge(*logit.filled("pv", t))
                    v.reciprocal(rden[:], heads[:, :, :, HD]).then_inc(rden_ready, 1)
                    wait(dve, x1_ready, t * 2)
                    dve.wait_ge(rden_ready, t + 1)
                    v.tensor_tensor(o[:].rearrange("p s (h d) -> p s h d", d=HD), heads[:, :, :, 0:HD],
                                    rden[:].unsqueeze(3).broadcast_to([P, NS, HEADS, HD]), ALU.mult
                                    ).then_inc(*logit.signal_emptied("pv", t))

                def rest(names):
                    for n in names:
                        j = int(n[4:])
                        dve.wait_ge(g_hi, u * FC + j + 1)
                        v.tensor_tensor(gT[1][:, j, :], whole[:, j % WHOLE, :], gT[0][:, j, :], ALU.subtract
                                        ).then_inc(g_ready, 1)

                def maxima(c):
                    dve.wait_ge(*logit.filled(f"s{c}", t))
                    v.tensor_reduce(nmax[:, c, :, :], lg[:].rearrange("p i (b m) -> p i b m", b=NB), AX.X, ALU.max,
                                    negate=True).then_inc(*logit.signal_emptied(f"s{c}", t))
                    dve.wait_ge(*logit.emptied(f"s{c}", t))
                    rest, three = nmax[:, c, :, :], nparts[:, c, :, :, :]
                    done = t * 8 + 4 * c
                    v.tensor_copy(three[:, 0, :, :], rest).then_inc(nmax_step, 1)
                    dve.wait_ge(nmax_step, done + 1)
                    v.tensor_tensor(rest, rest, three[:, 0, :, :], ALU.subtract).then_inc(nmax_step, 1)
                    dve.wait_ge(nmax_step, done + 2)
                    v.tensor_copy(three[:, 1, :, :], rest).then_inc(nmax_step, 1)
                    dve.wait_ge(nmax_step, done + 3)
                    v.tensor_tensor(three[:, 2, :, :], rest, three[:, 1, :, :], ALU.subtract).then_inc(nmax_step, 1)
                    dve.wait_ge(nmax_step, done + 4)
                    for j, r in ((0, slice(0, SEQ)), (1, slice(SEQ, P))):
                        last = v.tensor_copy(nmaxU[r, c, :, :, :, j], nparts[r, c, :, :, :].rearrange(
                            "p a i b -> p b a i"))
                    last.then_inc(nmaxU_ready, 1)

                def mlp_weights():
                    for k, (src, w) in enumerate(mlp_splits):
                        dve.wait_ge(w_hi, KC + 1 + k + 1)
                        v.tensor_tensor(w[1], src, w[0], ALU.subtract).then_inc(w_ready, 1)

                def scale_rows(tile, k):
                    dve.wait_ge(rms_ready, tile * 2 + k + 1)
                    for s in (2 * k, 2 * k + 1):
                        last = v.scalar_tensor_tensor(xo[:, s, :], xo[:, s, :], rms[:, s:s + 1], vec2[:, s, 1, :],
                                                      ALU.mult, ALU.mult)
                    last.then_inc(ys_ready, 1)

                def values(n):
                    dve.wait_ge(*gemm.filled(n, t))
                    halves_of = ((0, slice(0, SEQ)), (1, slice(SEQ, P)))
                    for h, r in halves_of:
                        for j, to in halves_of:
                            last = v.tensor_tensor(
                                v2[to, :, :, j, 0:HD].rearrange("p (a h) q d -> p a h q d", h=2)[
                                    :, 2 * int(n[1]):2 * int(n[1]) + 2, h, :, :],
                                gemm.bank(n, t)[r, :].rearrange("p (a q j d) -> p a q j d", a=2, j=2, d=HD)[
                                    :, :, :, j, :],
                                bv[r, :].rearrange("p (q j d) -> p q j d", j=2, d=HD)[:, :, j, :].unsqueeze(1)
                                .broadcast_to([SEQ, 2, PAIRS, HD]), ALU.add)
                    last.then_inc(*gemm.signal_emptied(n, t))

                if attn:
                    split("q0")
                    split("k0")
                if mlp:
                    dve.wait_ge(x1_ready, (u + 1) * 2)
                    statistics(u, x1, st2, mv2, ve2, nm2, ln2_step)
                if attn:
                    split("q1")
                if mlp:
                    normalised(u, (2, 3), x1, mv2, rs2, ln2_rstd, hn2_ready)
                if attn:
                    split("k1")
                    values("v0")
                if mlp:
                    dve.wait_ge(mod2_in, (u + 1) * 16)
                    columns([(lg[:, c, :], (h2_filled, u + 1), (h2_scaled, 1), (h2_scaled, u * KC + c + 1))
                             for c in range(KC)], mod2, hT2, hT2_hi)
                if mlp:
                    columns_rest(u, hT2, hT2_hi, hw2, hw2_ready, hT2_ready)
                if attn:
                    values("v1")
                if late:
                    rows_in(misc, "fc2_1", t, b2, mlp_rows[:, 2:4, :])
                if attn and not mlp:
                    dve.wait_ge(scratch_out, 16)
                if attn:
                    maxima(0)
                if late:
                    scale_rows(w, 0)
                if mlp:
                    rest(fc1_names[0:2])
                if attn:
                    maxima(1)
                if late:
                    scale_rows(w, 1)
                if more:
                    ln1(t + 1)
                if attn:
                    dve.wait_ge(*misc.filled("max1", t))
                    v.tensor_copy(nmaxT[:, 1, :], misc.bank("max1", t)[0:MAX_ROWS, :]
                                  ).then_inc(*misc.signal_emptied("max1", t))
                if mlp:
                    rest(fc1_names[2:3])
                if more:
                    ln1_rows(t + 1)
                if mlp:
                    rest(fc1_names[3:6])
                elif attn:
                    mlp_weights()
                if more:
                    columns_of_next(t)
                if mlp:
                    rest(fc1_names[6:8])
                if attn:
                    attended()
                if more:
                    columns_of_next_rest(t)
                if attn:
                    for c in range(KC):
                        dve.wait_ge(oT_hi, t * KC + c + 1)
                        v.tensor_tensor(oT[1][:, c, :], gemm.bank(f"oT{c}", t)[:], oT[0][:, c, :], ALU.subtract
                                        ).then_inc(*gemm.signal_emptied(f"oT{c}", t))
                if mlp:
                    rows_in(misc, "fc2_0", t, b2, mlp_rows[:, 0:2, :])
                if attn:
                    dve.wait_ge(*gemm.filled("oT0", t))
                    dve.wait_ge(*gemm.filled("oT1", t))
                    dve.wait_ge(gate1_in, (t + 1) * 32)
                    for k, n in enumerate(("proj0", "proj1")):
                        rows = o[:, 2 * k:2 * k + 2, :]
                        rows_in(gemm, n, t, bp, rows)
                        dve.wait_ge(*gemm.emptied(n, t))
                        v.tensor_tensor(rows, rows, gate1[:, 2 * k:2 * k + 2, :], ALU.mult).then_inc(attn_gated, 1)

            turns(dve, body)

        @block.gpsimd
        def _(pool):
            g = nc.gpsimd

            def power(src, dst, ready):
                g.tensor_tensor(dst, src, halves[:, 0:src.shape[1]], ALU.pow).then_inc(ready, 1)

            def shift_columns(t, mod, mod_in, scaled, hw, ready):
                pool.wait_ge(mod_in, (t + 1) * 16)
                for c in range(KC):
                    pool.wait_ge(*scaled[c])
                    g.tensor_tensor(hw[:, c, :].rearrange("p (b n) -> p b n", b=NB),
                                    hS[:, c, :].rearrange("p (b n) -> p b n", b=NB),
                                    mod[:, c, :].unsqueeze(2).broadcast_to([P, NB, SEQ]), ALU.add).then_inc(ready, 1)

            def gate_and_add(k, t, there, acc, gate, gated, res, dst, ready):
                s = slice(2 * k, 2 * k + 2)
                rows = acc[:, s, :]
                pool.wait_ge(*there)
                g.tensor_tensor(rows, rows, gate[:, s, :], ALU.mult).then_inc(gated, 1)
                pool.wait_ge(gated, t * 2 + k + 1)
                g.tensor_tensor(dst[:, s, :], res[:, s, :], rows, ALU.add).then_inc(ready, 1)

            def scale_and_shift(t, step, ve, rs, nm, rstd, shift):
                pool.wait_ge(step, (t + 1) * 3)
                power(ve[:], rs[:], rstd)
                pool.wait_ge(rstd, t + 1)
                g.tensor_tensor(nm[:], nm[:], rs[:], ALU.mult).then_inc(shift, 1)

            def next_rstd(turn):
                pool.wait_ge(ln1_step, (turn + 2) * 3)
                power(ve1[:], rs1[:], ln1_rstd)

            def next_columns(turn):
                shift_columns(turn + 1, mod1, mod1_in, [misc.emptied(n, turn) for n in ("h1_0", "h1_1")], hw1,
                              hw1_ready)

            pool.wait_ge(zeros_set, ZEROS_ALL)
            next_rstd(-1)
            next_columns(-1)

            def body(t, attn, mlp, late, more):
                u, w = t - 1, t - 2

                def mean_square(tile, k):
                    s = slice(2 * k, 2 * k + 2)
                    pool.wait_ge(ssq_ready, tile * NS + 2 * k + 2)
                    g.tensor_tensor(msq[:, s], ssq[:, s], epss[:, s], ALU.add).then_inc(msq_ready, 1)
                    pool.wait_ge(msq_ready, tile * 2 + k + 1)
                    power(msq[:, s], rms[:, s], rms_ready)

                def shift_rows(tile, k):
                    s = slice(2 * k, 2 * k + 2)
                    pool.wait_ge(ys_ready, tile * 2 + k + 1)
                    g.tensor_tensor(xo[:, s, :], xo[:, s, :], vec2[:, s, 2, :], ALU.add).then_inc(y_ready, 1)

                def rounded(dst, src):
                    width = src.shape[-1]
                    by = one[:].broadcast_to([P, width]) if len(src.shape) == 2 else (
                        one[:].unsqueeze(2).broadcast_to([P, src.shape[1], width]))
                    return g.tensor_tensor(dst, src, by, ALU.mult)

                def first_parts(names):
                    for n in names:
                        j = int(n[4:])
                        pool.wait_ge(*gemm.emptied(n, t))
                        rounded(gT[0][:, j, :], whole[:, j % WHOLE, :]).then_inc(g_hi, 1)

                def third_parts(names):
                    for n in names:
                        k = QK.index(n)
                        dst = (kparts if n[0] == "k" else qparts)[:, int(n[1]), :, :]
                        pool.wait_ge(mid_ready, t * 4 + k + 1)
                        g.tensor_tensor(dst[:, 2, :], whole[:, k, :], dst[:, 1, :], ALU.subtract
                                        ).then_inc(parts_ready, 1)

                if attn:
                    third_parts(("q0", "k0"))
                if mlp:
                    scale_and_shift(u, ln2_step, ve2, rs2, nm2, ln2_rstd, ln2_shift)
                if attn:
                    third_parts(("q1", "k1"))
                if mlp:
                    shift_columns(u, mod2, mod2_in, [(h2_scaled, u * KC + c + 1) for c in range(KC)], hw2, hw2_ready)
                if late:
                    pool.wait_ge(vec2_in, (w + 1) * 32)
                    pool.wait_ge(x1_kept, w + 1)
                    gate_and_add(0, w, misc.emptied("fc2_0", u), mlp_rows, vec2[:, :, 0, :], mlp_gated, xo, xo,
                                 x2_ready)
                    mean_square(w, 0)
                    gate_and_add(1, w, misc.emptied("fc2_1", t), mlp_rows, vec2[:, :, 0, :], mlp_gated, xo, xo,
                                 x2_ready)
                if mlp:
                    first_parts(fc1_names[0:2])
                if late:
                    shift_rows(w, 0)
                    mean_square(w, 1)
                if mlp:
                    first_parts(fc1_names[2:4])
                elif attn:
                    pool.wait_ge(mlp_weights_in, 48)
                    for src, (hi, _) in mlp_splits:
                        rounded(hi, src).then_inc(w_hi, 1)
                if late:
                    shift_rows(w, 1)
                if more:
                    next_rstd(t)
                if mlp:
                    first_parts(fc1_names[4:8])
                if more:
                    if mlp:
                        pool.wait_ge(g_ready, u * FC + WHOLE + KC)
                    next_columns(t)
                if attn:
                    pool.wait_ge(x_res_ready, t + 1)
                    if mlp:
                        pool.wait_ge(x1_kept, u + 1)
                    for k in range(2):
                        s = slice(2 * k, 2 * k + 2)
                        pool.wait_ge(attn_gated, t * 2 + k + 1)
                        g.tensor_tensor(x1[:, s, :], x_res[:, s, :], o[:, s, :], ALU.add).then_inc(x1_ready, 1)

            turns(pool, body)


W_SPLITS = 2 * KC + 3
STACK_LOADS = 16 * (len(Q_RUNS) + len(K_RUNS))
PREP_WABS, PREP_CQ, PREP_MODS, PREP_CQT, PREP_GATES, PREP_TOK, PREP_ALL = 6, 13, 21, 22, 23, 29, 29
ZEROS_ALL = 7
COND_ALL, CONSTS_ALL = 16 * 4, 16 * 7
MOD_COLS = [g * D + k * P for g in (0, 1, 3, 4) for k in range(KC)]


def kernel(x, cond_1024, L0_cond_W_qkv, L0_cond_b_qkv, L0_cond_W_proj, L0_cond_b_proj, L0_cond_W_fc1, L0_cond_b_fc1,
           L0_cond_W_fc2, L0_cond_b_fc2, L0_cond_W_ada, L0_cond_b_ada, L1_cond_w_proj, L1_cond_b_proj,
           L1_cond_rms_weight):
    import numpy as np
    import concourse.bacc as bacc
    from concourse.bass_utils import run_bass_kernel_spmd

    def chunks(w):
        w = np.asarray(w)
        return w.reshape(-1, P, w.shape[1]).transpose(1, 0, 2)

    def columns(b):
        return np.asarray(b).reshape(-1, P).T

    def line(b):
        return np.asarray(b).reshape(1, -1)

    ada_cols = columns(L0_cond_b_ada)
    mod_cols = [m // P for m in MOD_COLS]
    select = np.zeros((P, NI, P), np.float32)
    for a in range(3):
        for i in range(NI):
            for j in range(2):
                select[(a * NI + i) * 2 + j, i, j * SEQ:(j + 1) * SEQ] = 1.0
    arrays = {
        "x": np.asarray(x).reshape(BATCH * SEQ, D),
        "cT": chunks(np.asarray(cond_1024).T),
        "c": cond_1024,
        "w_qkv": chunks(L0_cond_W_qkv),
        "bT_qkv": columns(L0_cond_b_qkv)[:, 0:4],
        "b_v": line(L0_cond_b_qkv)[:, 2 * D:],
        "w_proj": chunks(L0_cond_W_proj),
        "b_proj": line(L0_cond_b_proj),
        "w_fc1": chunks(L0_cond_W_fc1),
        "bT_fc1": columns(L0_cond_b_fc1),
        "w_fc2": chunks(L0_cond_W_fc2),
        "b_fc2": line(L0_cond_b_fc2),
        "w_ada": chunks(L0_cond_W_ada),
        "bT_ada": ada_cols[:, mod_cols],
        "b_ada": line(L0_cond_b_ada),
        "w1T": chunks(np.asarray(L1_cond_w_proj).T),
        "b1": line(L1_cond_b_proj),
        "rms_w": line(L1_cond_rms_weight),
        "ident": np.eye(P, dtype=np.float32),
        "fold": np.tile(np.eye(SEQ, dtype=np.float32), (2, 1)),
        "select": select,
    }
    arrays = {k: np.ascontiguousarray(a) for k, a in arrays.items()}
    nc = bacc.Bacc("TRN2", target_bir_lowering=False, num_devices=1)
    args = {k: nc.dram_tensor(f"in_{k}", a.shape, mybir.dt.from_np(a.dtype), kind="ExternalInput").ap()
            for k, a in arrays.items()}
    result = nc.dram_tensor("out_rows", (BATCH * SEQ, D), F32, kind="ExternalOutput").ap()
    build(nc, out=result, **args)
    r = run_bass_kernel_spmd(nc, [{f"in_{k}": a for k, a in arrays.items()}], core_ids=[0])
    return r.results[0]["out_rows"].reshape(BATCH, SEQ, D)
```
